# Optimizing a Trainium2 kernel written in Bass

```python
import numpy as np
import jax
import jax.numpy as jnp

def _softmax(x, axis=-1):
    return jax.nn.softmax(x, axis=axis)

def _gelu(x):
    return jax.nn.gelu(x, approximate=True)

def _silu(x):
    return jax.nn.silu(x)

def _sigmoid(x):
    return jax.nn.sigmoid(x)

def _layernorm(x, axis=-1, eps=1e-05):
    m = jnp.mean(x, axis=axis, keepdims=True)
    v = jnp.var(x, axis=axis, keepdims=True)
    return (x - m) / jnp.sqrt(v + eps)

def _scatter_add(tgt, idx, src, axis=0):
    return tgt.at[idx].add(src)

def _segment_sum(src, seg, n):
    return jax.ops.segment_sum(src, seg, n)
kernel_name = 'mk_dlrm_tower_d1_rec_r8_64daf3'

def setup_inputs(seed: int=0):
    np.random.seed(seed)
    _w = jnp.asarray

    def _rec_inputs():
        import jax
        import jax.numpy as jnp
        _tk = jax.random.key(seed)
        ids = jnp.stack([jax.random.randint(jax.random.fold_in(_tk, 200 + f), (2048,), 0, v, jnp.int32) for f, v in enumerate([12500, 1250, 125000, 1000, 12500, 1000, 1000, 1000, 1000, 1250, 1250, 1000, 12500, 12500, 1250, 1000, 12500, 12500, 1000, 1250, 1000, 12500, 1250, 12500, 1250, 1250])], axis=1)
        tbl_0 = 0.05 * jax.random.normal(jax.random.fold_in(_tk, 500 + 0), (12500, 128), jnp.float32)
        tbl_1 = 0.05 * jax.random.normal(jax.random.fold_in(_tk, 500 + 1), (1250, 128), jnp.float32)
        tbl_2 = 0.05 * jax.random.normal(jax.random.fold_in(_tk, 500 + 2), (125000, 128), jnp.float32)
        tbl_3 = 0.05 * jax.random.normal(jax.random.fold_in(_tk, 500 + 3), (1000, 128), jnp.float32)
        tbl_4 = 0.05 * jax.random.normal(jax.random.fold_in(_tk, 500 + 4), (12500, 128), jnp.float32)
        tbl_5 = 0.05 * jax.random.normal(jax.random.fold_in(_tk, 500 + 5), (1000, 128), jnp.float32)
        tbl_6 = 0.05 * jax.random.normal(jax.random.fold_in(_tk, 500 + 6), (1000, 128), jnp.float32)
        tbl_7 = 0.05 * jax.random.normal(jax.random.fold_in(_tk, 500 + 7), (1000, 128), jnp.float32)
        tbl_8 = 0.05 * jax.random.normal(jax.random.fold_in(_tk, 500 + 8), (1000, 128), jnp.float32)
        tbl_9 = 0.05 * jax.random.normal(jax.random.fold_in(_tk, 500 + 9), (1250, 128), jnp.float32)
        tbl_10 = 0.05 * jax.random.normal(jax.random.fold_in(_tk, 500 + 10), (1250, 128), jnp.float32)
        tbl_11 = 0.05 * jax.random.normal(jax.random.fold_in(_tk, 500 + 11), (1000, 128), jnp.float32)
        tbl_12 = 0.05 * jax.random.normal(jax.random.fold_in(_tk, 500 + 12), (12500, 128), jnp.float32)
        tbl_13 = 0.05 * jax.random.normal(jax.random.fold_in(_tk, 500 + 13), (12500, 128), jnp.float32)
        tbl_14 = 0.05 * jax.random.normal(jax.random.fold_in(_tk, 500 + 14), (1250, 128), jnp.float32)
        tbl_15 = 0.05 * jax.random.normal(jax.random.fold_in(_tk, 500 + 15), (1000, 128), jnp.float32)
        tbl_16 = 0.05 * jax.random.normal(jax.random.fold_in(_tk, 500 + 16), (12500, 128), jnp.float32)
        tbl_17 = 0.05 * jax.random.normal(jax.random.fold_in(_tk, 500 + 17), (12500, 128), jnp.float32)
        tbl_18 = 0.05 * jax.random.normal(jax.random.fold_in(_tk, 500 + 18), (1000, 128), jnp.float32)
        tbl_19 = 0.05 * jax.random.normal(jax.random.fold_in(_tk, 500 + 19), (1250, 128), jnp.float32)
        tbl_20 = 0.05 * jax.random.normal(jax.random.fold_in(_tk, 500 + 20), (1000, 128), jnp.float32)
        tbl_21 = 0.05 * jax.random.normal(jax.random.fold_in(_tk, 500 + 21), (12500, 128), jnp.float32)
        tbl_22 = 0.05 * jax.random.normal(jax.random.fold_in(_tk, 500 + 22), (1250, 128), jnp.float32)
        tbl_23 = 0.05 * jax.random.normal(jax.random.fold_in(_tk, 500 + 23), (12500, 128), jnp.float32)
        tbl_24 = 0.05 * jax.random.normal(jax.random.fold_in(_tk, 500 + 24), (1250, 128), jnp.float32)
        tbl_25 = 0.05 * jax.random.normal(jax.random.fold_in(_tk, 500 + 25), (1250, 128), jnp.float32)
        _rk = jax.random.fold_in(_tk, 7)
        r_dense_output = -0.000520686 + 1.00062 * jax.random.normal(jax.random.fold_in(_rk, 101), (2048, 128), jnp.float32)
        W_top1 = 0.0405887 * jax.random.normal(jax.random.fold_in(_tk, 801), (607, 512), jnp.float32)
        W_top2 = 0.0441942 * jax.random.normal(jax.random.fold_in(_tk, 802), (512, 256), jnp.float32)
        W_top3 = 0.0625 * jax.random.normal(jax.random.fold_in(_tk, 803), (256, 1), jnp.float32)
        b_top1 = jnp.zeros((512,), jnp.float32)
        b_top2 = jnp.zeros((256,), jnp.float32)
        return (r_dense_output, ids, tbl_0, tbl_1, tbl_2, tbl_3, tbl_4, tbl_5, tbl_6, tbl_7, tbl_8, tbl_9, tbl_10, tbl_11, tbl_12, tbl_13, tbl_14, tbl_15, tbl_16, tbl_17, tbl_18, tbl_19, tbl_20, tbl_21, tbl_22, tbl_23, tbl_24, tbl_25, W_top1, b_top1, W_top2, b_top2, W_top3)
    r_dense_output, ids, tbl_0, tbl_1, tbl_2, tbl_3, tbl_4, tbl_5, tbl_6, tbl_7, tbl_8, tbl_9, tbl_10, tbl_11, tbl_12, tbl_13, tbl_14, tbl_15, tbl_16, tbl_17, tbl_18, tbl_19, tbl_20, tbl_21, tbl_22, tbl_23, tbl_24, tbl_25, W_top1, b_top1, W_top2, b_top2, W_top3 = _rec_inputs()

    def _L0_rec_setup():
        import jax, jax.numpy as jnp
        import numpy as np
        B, NUM_SPARSE, D = (2048, 26, 128)
        key = jax.random.key(seed)
        k1, k2 = jax.random.split(key)
        dense_output = jax.random.normal(k1, (B, D), dtype=jnp.float32)
        embeddings = jax.random.normal(k2, (B, NUM_SPARSE, D), dtype=jnp.float32)
        return {'dense_output': dense_output, 'embeddings': embeddings}
    _L0_rec_all = _L0_rec_setup()
    _L0_rec_in = {k: v for k, v in _L0_rec_all.items() if k in ()}
    del _L0_rec_all
    return {'r_dense_output': r_dense_output, 'ids': ids, 'tbl_0': tbl_0, 'tbl_1': tbl_1, 'tbl_2': tbl_2, 'tbl_3': tbl_3, 'tbl_4': tbl_4, 'tbl_5': tbl_5, 'tbl_6': tbl_6, 'tbl_7': tbl_7, 'tbl_8': tbl_8, 'tbl_9': tbl_9, 'tbl_10': tbl_10, 'tbl_11': tbl_11, 'tbl_12': tbl_12, 'tbl_13': tbl_13, 'tbl_14': tbl_14, 'tbl_15': tbl_15, 'tbl_16': tbl_16, 'tbl_17': tbl_17, 'tbl_18': tbl_18, 'tbl_19': tbl_19, 'tbl_20': tbl_20, 'tbl_21': tbl_21, 'tbl_22': tbl_22, 'tbl_23': tbl_23, 'tbl_24': tbl_24, 'tbl_25': tbl_25, 'W_top1': W_top1, 'b_top1': b_top1, 'W_top2': W_top2, 'b_top2': b_top2, 'W_top3': W_top3}

def reference(r_dense_output, ids, tbl_0, tbl_1, tbl_2, tbl_3, tbl_4, tbl_5, tbl_6, tbl_7, tbl_8, tbl_9, tbl_10, tbl_11, tbl_12, tbl_13, tbl_14, tbl_15, tbl_16, tbl_17, tbl_18, tbl_19, tbl_20, tbl_21, tbl_22, tbl_23, tbl_24, tbl_25, W_top1, b_top1, W_top2, b_top2, W_top3):
    import jax
    import jax.numpy as jnp

    def _L0_rec_ref(dense_output, embeddings):
        import jax, jax.numpy as jnp
        import numpy as np
        B, NUM_SPARSE, D = (2048, 26, 128)
        combined = jnp.concatenate([dense_output[:, None, :], embeddings], axis=1)
        interactions = jnp.einsum('bfd,bgd->bfg', combined, combined)
        F = combined.shape[1]
        iu, ju = jnp.triu_indices(F, k=1)
        interactions_flat = interactions[:, iu, ju]
        return jnp.concatenate([dense_output, interactions_flat], axis=1)
    e = jnp.stack([tbl_0[ids[:, 0]], tbl_1[ids[:, 1]], tbl_2[ids[:, 2]], tbl_3[ids[:, 3]], tbl_4[ids[:, 4]], tbl_5[ids[:, 5]], tbl_6[ids[:, 6]], tbl_7[ids[:, 7]], tbl_8[ids[:, 8]], tbl_9[ids[:, 9]], tbl_10[ids[:, 10]], tbl_11[ids[:, 11]], tbl_12[ids[:, 12]], tbl_13[ids[:, 13]], tbl_14[ids[:, 14]], tbl_15[ids[:, 15]], tbl_16[ids[:, 16]], tbl_17[ids[:, 17]], tbl_18[ids[:, 18]], tbl_19[ids[:, 19]], tbl_20[ids[:, 20]], tbl_21[ids[:, 21]], tbl_22[ids[:, 22]], tbl_23[ids[:, 23]], tbl_24[ids[:, 24]], tbl_25[ids[:, 25]]], axis=1)
    z = _L0_rec_ref(r_dense_output, e)
    z = z.reshape(z.shape[0], -1)
    h = jnp.concatenate([z, r_dense_output], axis=1)
    h = jnp.maximum(h @ W_top1 + b_top1, 0.0)
    h = jnp.maximum(h @ W_top2 + b_top2, 0.0)
    y = h @ W_top3
    return y

_drawn_inputs = setup_inputs


def setup_inputs(seed=0):
    import zlib

    import numpy as np

    out = dict(_drawn_inputs(seed))
    spreads = {'b_top1': (0.0, 0.1), 'b_top2': (0.0, 0.1)}
    factors = {}
    for name, (base, spread) in spreads.items():
        noise = np.random.default_rng([zlib.crc32(name.encode()), seed]).standard_normal(out[name].shape)
        drawn = base * np.exp(spread * noise) if base else spread * noise
        out[name] = jnp.asarray(drawn.astype(out[name].dtype))
    for name, factor in factors.items():
        out[name] = (out[name] * factor).astype(out[name].dtype)
    return out
```

```python
from contextlib import ExitStack

import concourse.bass as bass
import numpy as np
from concourse import mybir

P = 128
B, D = 2048, 128
TABLES = 26
SLOTS = TABLES + 1
TILES = B // P
BLOCK_TILES = 4
BLOCKS = TILES // BLOCK_TILES
BLOCK = BLOCK_TILES * P
PAIR = 2 * P

ONEHOT_TABLES = [3, 5, 6, 7, 8, 11]
GATHERED = [t for t in range(TABLES) if t not in ONEHOT_TABLES]
ONE, GATH = len(ONEHOT_TABLES), len(GATHERED)
SLOT_TABLES = GATHERED + ONEHOT_TABLES
VOCAB = 1000
CHUNKS = 8
CHUNK_ROWS = VOCAB // CHUNKS
HALF = CHUNKS // 2
ONEHOT_BUFFERS = 3

TR_SLOTS = 1 + GATH
TR_GROUPS = [range(s, min(s + 4, TR_SLOTS)) for s in range(0, TR_SLOTS, 4)]

SHARE = 4
QUADS = P // SHARE
GRAM_UNIT = 8
UNITS = QUADS // GRAM_UNIT
PAIRS = SLOTS * (SLOTS - 1) // 2
KP = PAIRS // 3
H1, H2 = 512, 256
N1, N2 = H1 // P, H2 // P
STRIDE = P // SHARE

SLOT_BANKS = 3
_turns = []
for _h in range(2):
    _turns += [("slots", 2 * _h, g) for g in range(len(TR_GROUPS))]
    _turns += [("onehot", _h, u) for u in range(ONE)]
    _turns += [("slots", 2 * _h + 1, g) for g in range(len(TR_GROUPS))]
_turns += [("pairsT", k) for k in range(3)] + [("h2", m) for m in range(N2)] + [("y",)]
UNITS_OF_BLOCK = [(t, u) for t in range(BLOCK_TILES) for u in range(UNITS)]
_pair_turns = [("gram", t, u) for t, u in UNITS_OF_BLOCK] + [("pairs", n) for n in range(4)]
_pair_turns += [("h1", n) for n in range(2)]
USES = {f"bank{k}": _turns[k::SLOT_BANKS] for k in range(SLOT_BANKS)}
USES |= {f"banks{k}": _pair_turns[k::2] for k in range(2)}
BANK_OF = {use: (m, int(m[-1])) for m in USES for use in USES[m]}


def pair_base(a):
    return a * SLOTS - a * (a + 1) // 2


def unit_slots(n):
    slots = list(range(8 * n, min(8 * n + 8, SLOTS - 1)))
    half = len(slots) // 2
    return [(a, k if k < half else 4 + k - half) for k, a in enumerate(slots)]


def build(nc, dense, ids, ids_t, tables, w1, b1, w2, b2, w3, y):
    f32, f32r, i32 = mybir.dt.float32, mybir.dt.float32r, mybir.dt.int32
    ALU = mybir.AluOpType
    ACT = mybir.ActivationFunctionType

    dense_v = dense.rearrange("(p t) d -> p t d", t=TILES)
    ids_v = ids.rearrange("(p t) f -> p t f", t=TILES)

    ctx = ExitStack()
    with ctx:
        def sb(name, shape, dt=f32):
            return ctx.enter_context(nc.sbuf_tensor(name, shape, dt))

        def sem(name):
            return ctx.enter_context(nc.semaphore(name))

        emb = sb("emb", [P, BLOCK_TILES, TR_SLOTS, D])
        emb_t = sb("emb_t", [P, 2, P, STRIDE])
        ids_sb = sb("ids_sb", [P, BLOCK_TILES, TABLES], i32)
        hi = sb("hi", [CHUNK_ROWS, ONE, CHUNKS, D], f32r)
        lo = sb("lo", [CHUNK_ROWS, ONE, CHUNKS, D], f32r)
        onehot = sb("onehot", [CHUNK_ROWS, ONEHOT_BUFFERS, HALF, PAIR], f32r)
        ids_f = sb("ids_f", [ONE, B], f32r)
        ids_raw = sb("ids_raw", [ONE, B], i32)
        pick = sb("pick", [ONE, ONE, P], f32r)
        row_i = sb("row_i", [P, CHUNKS], i32)
        row_f = sb("row_f", [P, CHUNKS])
        ident = sb("ident", [P, P])
        gram = sb("gram", [P, BLOCK_TILES, QUADS, SLOTS])
        pairs = sb("pairs", [P, SHARE, PAIRS])
        pairs_t = sb("pairs_t", [KP, 3, BLOCK])
        dense_t = sb("dense_t", [P, BLOCK])
        w1_sb = sb("w1_sb", [P, 4, H1])
        w2_sb = sb("w2_sb", [P, N1, H2])
        w3_sb = sb("w3_sb", [P, N2])
        b1_sb = sb("b1_sb", [P, N1])
        b2_sb = sb("b2_sb", [P, N2])
        h1 = sb("h1", [P, N1, BLOCK])
        h2 = sb("h2", [P, N2, BLOCK])
        w1_again = h2[:, 0, :]
        y_sb = ids_raw[0:1, :].bitcast(f32)
        raw = emb[0:CHUNK_ROWS, 1:BLOCK_TILES, :, :].rearrange("p a s d -> p (a s d)")[:, 0:ONE * CHUNKS * D]\
            .rearrange("p (k c d) -> p k c d", k=ONE, c=CHUNKS)

        bank_ps = [ctx.enter_context(nc.psum_tensor(f"bank_ps{k}", [P, 4, P], f32)) for k in range(SLOT_BANKS)]
        ids_ps = ctx.enter_context(nc.psum_tensor("ids_ps", [P, 2, PAIR], f32))
        gram_ps = [ctx.enter_context(nc.psum_tensor(f"gram_ps{k}", [P, GRAM_UNIT, P], f32)) for k in range(2)]

        ids_ready = [sem(f"ids_ready{i}") for i in range(BLOCK_TILES)]
        dense_ready = [sem(f"dense_ready{i}") for i in range(BLOCK_TILES)]
        gathered = [sem(f"gathered{i}") for i in range(BLOCK_TILES)]
        raw_ready = [sem(f"raw_ready{k}") for k in range(ONE)]
        ids_t_ready = sem("ids_t_ready")
        weights_ready = sem("weights_ready")
        hi_made = sem("hi_made")
        lo_made = sem("lo_made")
        ids_f_made = sem("ids_f_made")
        zeroed = sem("zeroed")
        consts_made = sem("consts_made")
        rows_made = sem("rows_made")
        pads_made = sem("pads_made")
        w1_summed = sem("w1_summed")
        ids_spread = sem("ids_spread")
        onehot_ready = sem("onehot_ready")
        onehot_used = sem("onehot_used")
        y_stored = sem("y_stored")
        gather_begun, spread_begun = sem("gather_begun"), sem("spread_begun")
        full = {m: sem(f"{m}_full") for m in USES}
        taken = {m: sem(f"{m}_taken") for m in USES}
        takers = {m: 2 if m.startswith("banks") else 1 for m in USES}
        filled = {m: [use for use in USES[m] if use[0] != "onehot"] for m in USES}

        def wait_full(eng, b, use):
            m, _ = BANK_OF[use]
            eng.wait_ge(full[m], b * len(filled[m]) + (filled[m].index(use) + 1))

        def wait_empty(eng, b, use):
            m, _ = BANK_OF[use]
            eng.wait_ge(taken[m], b * (takers[m] * len(USES[m])) + takers[m] * (USES[m].index(use) + 1))

        def wait_taken(eng, b, use):
            m, _ = BANK_OF[use]
            eng.wait_ge(taken[m], b * (takers[m] * len(USES[m])) + takers[m] * (USES[m].index(use) + 2))

        def bank(use):
            m, k = BANK_OF[use]
            return bank_ps[k], full[m], taken[m]

        def banks(use):
            m, k = BANK_OF[use]
            return gram_ps[k], full[m], taken[m]

        def row(ps):
            return ps.rearrange("n g c -> n (g c)")

        def emb_view(k):
            return emb_t[:, k, :, 0:SLOTS]

        block = ctx.enter_context(nc.Block())

        @block.sync
        def _(sp):
            def load_tile(t, i):
                sp.dma_start(ids_sb[:, i:i + 1, :], ids_v[:, bass.ds(t, 1), :]).then_inc(ids_ready[i], 16)
                sp.dma_start(emb[:, i, 0:1, :], dense_v[:, bass.ds(t, 1), :]).then_inc(dense_ready[i], 16)

            for i in range(BLOCK_TILES):
                if i == 1:
                    sp.wait_ge(hi_made, ONE)
                    sp.wait_ge(lo_made, ONE)
                load_tile(i, i)
            with sp.Fori(1, BLOCKS) as b:
                for i in range(BLOCK_TILES):
                    wait_taken(sp, b - 1, ("slots", i, len(TR_GROUPS) - 1))
                    load_tile(b * BLOCK_TILES + i, i)
            wait_taken(sp, BLOCKS - 1, ("y",))
            sp.dma_start(y.rearrange("(a n) o -> a (n o)", a=1), y_sb).then_inc(y_stored, 16)
            sp.wait_ge(y_stored, 16)

        @block.gpsimd
        def _(pool):
            pool.memset(ident[:, :], 0.0).then_inc(zeroed, 1)
            pool.memset(pick[:, :, :].bitcast(f32), 0.0).then_inc(zeroed, 1)
            pool.iota(row_i[:, :], pattern=[[1, CHUNKS]], base=0, channel_multiplier=CHUNKS).then_inc(consts_made, 1)
            pool.wait_ge(zeroed, 2)
            pool.affine_select(out=ident[:, :], in_=ident[:, :], compare_op=ALU.not_equal, fill=1.0, base=0,
                               pattern=[[-1, P]], channel_multiplier=1).then_inc(consts_made, 1)
            pool.affine_select(out=pick[:, :, :], in_=pick[:, :, :].bitcast(f32), compare_op=ALU.not_equal, fill=1.0,
                               base=0, pattern=[[-1, ONE], [0, P]], channel_multiplier=1).then_inc(consts_made, 1)
            with pool.Fori(0, BLOCKS) as b:
                for i in range(BLOCK_TILES):
                    pool.wait_ge(ids_ready[i], b * 16 + 16)
                    pool.sem_inc(gather_begun, 1)
                    for s, t in enumerate(GATHERED):
                        pool.indirect_dma_start(
                            emb[:, i, 1 + s, :], None, tables[t],
                            bass.IndirectOffsetOnAxis(ap=ids_sb[:, i, t:t + 1], axis=0),
                        ).then_inc(gathered[i], 16)

        @block.scalar
        def _(act):
            for k, t in enumerate(ONEHOT_TABLES):
                act.dma_start(raw[:, k, :, :], tables[t].rearrange("(p c) d -> p c d", c=CHUNKS))\
                   .then_inc(raw_ready[k], 16)
                if k == 0:
                    act.dma_start(ids_raw[:, :], ids_t).then_inc(ids_t_ready, 16)
            act.dma_start(w1_sb[:, 0, :], w1[0:D, :]).then_inc(weights_ready, 16)
            act.dma_start(w1_again, w1[D + PAIRS:D + PAIRS + D, :]).then_inc(weights_ready, 16)
            act.dma_start(w1_sb[0:KP, 1:4, :], w1[D:D + PAIRS, :].rearrange("(k p) n -> p k n", p=KP))\
               .then_inc(weights_ready, 16)
            act.dma_start(w2_sb[:, :, :], w2.rearrange("(k p) n -> p k n", p=P)).then_inc(weights_ready, 16)
            with nc.allow_non_contiguous_dma("short vectors onto partitions"):
                act.dma_start(w3_sb[:, :], w3.rearrange("(k p) o -> p (k o)", p=P)).then_inc(weights_ready, 16)
                act.dma_start(b1_sb[:, :], b1.rearrange("(k p) -> p k", p=P)).then_inc(weights_ready, 16)
                act.dma_start(b2_sb[:, :], b2.rearrange("(k p) -> p k", p=P)).then_inc(weights_ready, 16)
            for k in range(ONE):
                act.wait_ge(raw_ready[k], 16)
                act.activation(hi[:, k, :, :], raw[:, k, :, :], ACT.Copy).then_inc(hi_made, 1)
            act.wait_ge(weights_ready, 7 * 16)

            with act.Fori(0, BLOCKS) as b:
                def take_onehot(h, u):
                    ps, _, free = bank(("onehot", h, u))
                    act.wait_ge(onehot_used, b * (4 * ONE) + (ONEHOT_BUFFERS + 2 * (h * ONE + u) + 2))
                    act.activation(emb_t[:, :, :, TR_SLOTS + u], ps[:, 0:2, :], ACT.Copy).then_inc(free, 1)

                def take_slots(i):
                    for g, slots in enumerate(TR_GROUPS):
                        use = ("slots", i, g)
                        ps, _, free = bank(use)
                        wait_full(act, b, use)
                        if g == 0:
                            act.activation(dense_t[:, i * P:(i + 1) * P], ps[:, 0, :], ACT.Copy)
                        n = len(slots)
                        act.activation(emb_view(i % 2)[:, :, slots[0]:slots[0] + n],
                                       ps[:, 0:n, :].rearrange("d f p -> d p f"), ACT.Copy).then_inc(free, 1)

                def take_gram(i, u):
                    use = ("gram", i, u)
                    ps, _, free = banks(use)
                    wait_full(act, b, use)
                    for j in (0, 1):
                        last = act.activation(
                            gram[32 * j:32 * j + 32, i, u * GRAM_UNIT:(u + 1) * GRAM_UNIT, :],
                            ps[32 * j:32 * j + 32, :, j * SLOTS:(j + 1) * SLOTS], ACT.Copy)
                    last.then_inc(free, 1)

                for h in range(2):
                    take_slots(2 * h)
                    for u in range(ONE):
                        take_onehot(h, u)
                    for u in range(UNITS // 2):
                        take_gram(2 * h, u)
                    take_slots(2 * h + 1)
                    for u in range(UNITS // 2, UNITS):
                        take_gram(2 * h, u)
                    for u in range(UNITS):
                        take_gram(2 * h + 1, u)
                for n in range(4):
                    ps, _, free = banks(("pairs", n))
                    wait_full(act, b, ("pairs", n))
                    for a, at in (x for x in unit_slots(n) if x[1] < 4):
                        last = act.activation(
                            pairs[:, :, pair_base(a):pair_base(a + 1)],
                            ps[:, at, :].rearrange("q (j f) -> q j f", j=SHARE)[:, :, a + 1:SLOTS], ACT.Copy)
                    last.then_inc(free, 1)
                ps, _, free = bank(("pairsT", 1))
                wait_full(act, b, ("pairsT", 1))
                act.activation(pairs_t[:, 1, :].rearrange("k (q j) -> k q j", j=SHARE),
                               ps[0:KP, :, :].rearrange("k j q -> k q j"), ACT.Copy).then_inc(free, 1)
                for n in range(2):
                    ps, _, free = banks(("h1", n))
                    wait_full(act, b, ("h1", n))
                    act.activation(h1[:, 2 * n, :], row(ps[:, 0:4, :]), ACT.Relu,
                                   bias=b1_sb[:, 2 * n:2 * n + 1]).then_inc(free, 1)
                ps, _, free = bank(("h2", 0))
                wait_full(act, b, ("h2", 0))
                act.activation(h2[:, 0, :], row(ps[:, :, :]), ACT.Relu, bias=b2_sb[:, 0:1]).then_inc(free, 1)
                ps, _, free = bank(("y",))
                wait_full(act, b, ("y",))
                act.activation(
                    y_sb.rearrange("o (p t) -> o p t", t=TILES)[:, :, bass.ds(b * BLOCK_TILES, BLOCK_TILES)],
                    ps[0:1, :, :].rearrange("o t p -> o p t"), ACT.Copy).then_inc(free, 1)

        @block.vector
        def _(dve):
            dve.memset(emb_t[:, :, :, SLOTS:STRIDE], 0.0).then_inc(pads_made, 1)
            dve.wait_ge(consts_made, 3)
            dve.tensor_copy(row_f[:, :], row_i[:, :]).then_inc(rows_made, 1)
            dve.wait_ge(ids_t_ready, 16)
            dve.tensor_copy(ids_f[:, :], ids_raw[:, :]).then_inc(ids_f_made, 1)
            for k in range(ONE):
                dve.wait_ge(hi_made, k + 1)
                dve.tensor_tensor(lo[:, k, :, :], raw[:, k, :, :], hi[:, k, :, :].bitcast(f32), ALU.subtract)\
                   .then_inc(lo_made, 1)
            dve.wait_ge(weights_ready, 7 * 16)
            dve.tensor_tensor(w1_sb[:, 0, :], w1_sb[:, 0, :], w1_again, ALU.add).then_inc(w1_summed, 1)
            dve.wait_ge(rows_made, 1)

            with dve.Fori(0, BLOCKS) as b:
                def make_onehot(h, u):
                    if u % 2 == 0:
                        dve.wait_ge(ids_spread, b * ONE + (h * ONE + u) // 2 + 1)
                    for s in range(2):
                        n = (h * ONE + u) * 2 + s
                        dve.wait_ge(onehot_used, b * (4 * ONE) + (n + 1))
                        dve.tensor_tensor(
                            onehot[:, n % ONEHOT_BUFFERS, :, :],
                            ids_ps[0:CHUNK_ROWS, u % 2, :].unsqueeze(1).to_broadcast([CHUNK_ROWS, HALF, PAIR]),
                            row_f[0:CHUNK_ROWS, s * HALF:(s + 1) * HALF].unsqueeze(2)
                            .to_broadcast([CHUNK_ROWS, HALF, PAIR]),
                            ALU.is_equal).then_inc(onehot_ready, 1)

                def take_gram(i, u):
                    use = ("gram", i, u)
                    ps, _, free = banks(use)
                    wait_full(dve, b, use)
                    for j in (2, 3):
                        last = dve.tensor_copy(
                            gram[32 * j:32 * j + 32, i, u * GRAM_UNIT:(u + 1) * GRAM_UNIT, :],
                            ps[32 * j:32 * j + 32, :, j * SLOTS:(j + 1) * SLOTS])
                    last.then_inc(free, 1)

                for h in range(2):
                    for u in range(ONE):
                        make_onehot(h, u)
                    for i in (2 * h, 2 * h + 1):
                        for u in range(UNITS):
                            take_gram(i, u)
                for n in range(4):
                    ps, _, free = banks(("pairs", n))
                    wait_full(dve, b, ("pairs", n))
                    for a, at in (x for x in unit_slots(n) if x[1] >= 4):
                        last = dve.tensor_copy(
                            pairs[:, :, pair_base(a):pair_base(a + 1)],
                            ps[:, at, :].rearrange("q (j f) -> q j f", j=SHARE)[:, :, a + 1:SLOTS])
                    last.then_inc(free, 1)
                for k in (0, 2):
                    ps, _, free = bank(("pairsT", k))
                    wait_full(dve, b, ("pairsT", k))
                    dve.tensor_copy(pairs_t[:, k, :].rearrange("k (q j) -> k q j", j=SHARE),
                                    ps[0:KP, :, :].rearrange("k j q -> k q j")).then_inc(free, 1)
                for n in range(2):
                    ps, _, free = banks(("h1", n))
                    wait_full(dve, b, ("h1", n))
                    dve.tensor_scalar(h1[:, 2 * n + 1, :], row(ps[:, 4:8, :]), b1_sb[:, 2 * n + 1:2 * n + 2], 0.0,
                                      ALU.add, ALU.max).then_inc(free, 1)
                ps, _, free = bank(("h2", 1))
                wait_full(dve, b, ("h2", 1))
                dve.tensor_scalar(h2[:, 1, :], row(ps[:, :, :]), b2_sb[:, 1:2], 0.0, ALU.add, ALU.max)\
                   .then_inc(free, 1)

        @block.tensor
        def _(pe):
            for m in USES:
                pe.sem_inc(taken[m], takers[m])
            pe.sem_inc(onehot_used, ONEHOT_BUFFERS)
            pe.sem_inc(onehot_ready, 1)
            pe.wait_ge(consts_made, 3)
            pe.wait_ge(ids_f_made, 1)
            pe.wait_ge(pads_made, 1)

            with pe.Fori(0, BLOCKS) as b:
                def spread_ids(h, u):
                    pe.wait_ge(onehot_ready, b * (4 * ONE) + (1 + 2 * (h * ONE + u)))
                    pe.sem_inc(spread_begun, 1)
                    for k in range(2):
                        last = pe.matmul(ids_ps[:, k, :], pick[:, u + k, :],
                                         ids_f[:, bass.ds(b * BLOCK + h * PAIR, PAIR)], start=True, stop=True)
                    last.then_inc(ids_spread, 1)

                def onehot_gather(h, u):
                    use = ("onehot", h, u)
                    ps, _, _ = bank(use)
                    wait_empty(pe, b, use)
                    for s in range(2):
                        n = (h * ONE + u) * 2 + s
                        pe.wait_ge(onehot_ready, b * (4 * ONE) + (n + 2))
                        for c in range(HALF):
                            for part in (hi, lo):
                                chunk = s * HALF + c
                                last = pe.matmul(row(ps[:, 0:2, :]), part[:, u, chunk, :], onehot[:, n % ONEHOT_BUFFERS, c, :],
                                                 start=chunk == 0 and part is hi,
                                                 stop=chunk == CHUNKS - 1 and part is lo)
                        last.then_inc(onehot_used, 1)

                def transpose_tile(i):
                    pe.wait_ge(gathered[i], b * (16 * GATH) + 16 * GATH)
                    pe.wait_ge(dense_ready[i], b * 16 + 16)
                    for g, slots in enumerate(TR_GROUPS):
                        use = ("slots", i, g)
                        ps, ready, _ = bank(use)
                        wait_empty(pe, b, use)
                        for s in slots:
                            last = pe.transpose(ps[:, s - slots[0], :], emb[:, i, s, :], ident[:, :])
                        last.then_inc(ready, 1)

                def gram_products(i, u):
                    use = ("gram", i, u)
                    ps, ready, _ = banks(use)
                    wait_empty(pe, b, use)
                    for k in range(GRAM_UNIT):
                        at = (u * GRAM_UNIT + k) * SHARE
                        quad = emb_t[:, i % 2, at:at + SHARE, :]
                        last = pe.matmul(ps[:, k, 0:SHARE * SLOTS], quad.rearrange("d j f -> d (j f)"),
                                         quad[:, :, 0:SLOTS], start=True, stop=True)
                    last.then_inc(ready, 1)

                def tile_ready(i):
                    for g in range(len(TR_GROUPS))[-SLOT_BANKS:]:
                        wait_taken(pe, b, ("slots", i, g))

                for h in range(2):
                    spread_ids(h, 0)
                    transpose_tile(2 * h)
                    if h == 0:
                        pe.wait_ge(lo_made, ONE)
                    for u in range(ONE):
                        onehot_gather(h, u)
                        if u % 2 == 0 and u + 2 < ONE:
                            spread_ids(h, u + 2)
                    tile_ready(2 * h)
                    for u in range(ONE)[-SLOT_BANKS:]:
                        wait_taken(pe, b, ("onehot", h, u))
                    for u in range(UNITS // 2):
                        gram_products(2 * h, u)
                    transpose_tile(2 * h + 1)
                    for u in range(UNITS // 2, UNITS):
                        gram_products(2 * h, u)
                    tile_ready(2 * h + 1)
                    for u in range(UNITS):
                        gram_products(2 * h + 1, u)

                for u in (UNITS - 2, UNITS - 1):
                    wait_taken(pe, b, ("gram", BLOCK_TILES - 1, u))
                for n in range(4):
                    ps, ready, _ = banks(("pairs", n))
                    wait_empty(pe, b, ("pairs", n))
                    for a, at in unit_slots(n):
                        last = pe.transpose(ps[:, at, :], gram[:, :, :, a].rearrange("f t q -> f (t q)"),
                                            ident[:, :])
                    last.then_inc(ready, 1)
                h1_ps = [row(banks(("h1", n // 2))[0][:, 4 * (n % 2):4 * (n % 2) + 4, :]) for n in range(N1)]
                pe.wait_ge(w1_summed, 1)
                for n in range(N1):
                    if n % 2 == 0:
                        wait_empty(pe, b, ("h1", n // 2))
                    pe.matmul(h1_ps[n], w1_sb[:, 0, n * P:(n + 1) * P], dense_t[:, :], start=True, stop=False)
                for k in range(3):
                    ps, ready, _ = bank(("pairsT", k))
                    wait_empty(pe, b, ("pairsT", k))
                    for j in range(SHARE):
                        last = pe.transpose(ps[0:KP, j, :], pairs[:, j, k * KP:(k + 1) * KP], ident[:, :])
                    last.then_inc(ready, 1)
                for k in range(3):
                    wait_taken(pe, b, ("pairsT", k))
                    for n in range(N1):
                        last = pe.matmul(h1_ps[n], w1_sb[0:KP, 1 + k, n * P:(n + 1) * P], pairs_t[:, k, :],
                                         start=False, stop=k == 2)
                        if k == 2 and n % 2:
                            last.then_inc(banks(("h1", n // 2))[1], 1)
                for m in range(N2):
                    ps, ready, _ = bank(("h2", m))
                    wait_empty(pe, b, ("h2", m))
                    for k in range(N1):
                        if m == 0 and k % 2 == 0:
                            wait_taken(pe, b, ("h1", k // 2))
                        last = pe.matmul(row(ps[:, :, :]), w2_sb[:, k, m * P:(m + 1) * P], h1[:, k, :],
                                         start=k == 0, stop=k == N1 - 1)
                    last.then_inc(ready, 1)
                ps, ready, _ = bank(("y",))
                wait_empty(pe, b, ("y",))
                for m in range(N2):
                    wait_taken(pe, b, ("h2", m))
                    last = pe.matmul(row(ps[0:1, :, :]), w3_sb[:, m:m + 1], h2[:, m, :], start=m == 0,
                                     stop=m == N2 - 1)
                last.then_inc(ready, 1)


def kernel(**inputs):
    import concourse.bacc as bacc
    from concourse.bass_utils import run_bass_kernel_spmd

    nc = bacc.Bacc("TRN2", target_bir_lowering=False, num_devices=1)
    arrays = {}

    def give(name, a):
        a = np.ascontiguousarray(a)
        arrays[name] = a
        return nc.dram_tensor(name, a.shape, mybir.dt.from_np(a.dtype), kind="ExternalInput").ap()

    ids = np.asarray(inputs["ids"])
    w1 = np.asarray(inputs["W_top1"])
    slot_feature = [0] + [1 + t for t in SLOT_TABLES]
    order = []
    for a in range(SLOTS - 1):
        for c in range(a + 1, SLOTS):
            f, g = sorted((slot_feature[a], slot_feature[c]))
            order.append(D + f * SLOTS - f * (f + 1) // 2 + g - f - 1)
    w1 = w1[np.r_[0:D, order, D + PAIRS:D + PAIRS + D]]
    ids_t = ids[:, ONEHOT_TABLES].reshape(P, TILES, ONE).transpose(2, 1, 0).reshape(ONE, B)
    args = [give("dense", inputs["r_dense_output"]), give("ids", ids), give("ids_t", ids_t)]
    args.append([give(f"table{t}", inputs[f"tbl_{t}"]) for t in range(TABLES)])
    args += [give("w1", w1), give("b1", inputs["b_top1"]), give("w2", inputs["W_top2"]),
             give("b2", inputs["b_top2"]), give("w3", inputs["W_top3"])]
    y = nc.dram_tensor("y", (B, 1), mybir.dt.float32, kind="ExternalOutput").ap()
    build(nc, *args, y)
    r = run_bass_kernel_spmd(nc, [arrays], core_ids=[0])
    return r.results[0]["y"]
```

```python
from contextlib import ExitStack

import concourse.bass as bass
import numpy as np
from concourse import mybir

P = 128
B, D = 2048, 128
TABLES = 26
SLOTS = TABLES + 1
TILES = B // P
BLOCK_TILES = 4
BLOCKS = TILES // BLOCK_TILES
BLOCK = BLOCK_TILES * P
PAIR = 2 * P

ONEHOT_TABLES = [3, 5, 6, 7, 8, 11]
GATHERED = [t for t in range(TABLES) if t not in ONEHOT_TABLES]
ONE, GATH = len(ONEHOT_TABLES), len(GATHERED)
SLOT_TABLES = GATHERED + ONEHOT_TABLES
VOCAB = 1000
CHUNKS = 8
CHUNK_ROWS = VOCAB // CHUNKS
HALF = CHUNKS // 2
HALVES = 2
ONEHOT_BUFFERS = 3
UNITS_OH = 2 * ONE
FILLS = UNITS_OH // 2
START_FILLS = ONE // 2 + 1
assert ONE == 6, "the order of the steps below counts on it"
BESIDE = [ONE - 2, ONE - 4]

TR_SLOTS = 1 + GATH
TR_GROUPS = [range(s, min(s + 4, TR_SLOTS)) for s in range(0, TR_SLOTS, 4)]

SHARE = 4
STRIDE = P // SHARE
SIDE = SLOTS - 1
ROWS = STRIDE * (SHARE - 1) + SIDE
QUADS = P // SHARE
GRAM_UNIT = 8
UNITS = QUADS // GRAM_UNIT
PAIRS = SLOTS * (SLOTS - 1) // 2
COLUMNS = -(-(PAIRS + 1) // 3) * 3
KP = COLUMNS // 3
H1, H2 = 512, 256
N1 = H1 // P

PARTS = {False: {1: (0, BLOCK_TILES)}, True: {0: (0, 2), 1: (2, 2)}}
PAIR_UNITS = 4
SPLIT_PRODUCTS = [(0, 0), (1, 0), (0, 1)]

BANKS = 3


def turns(last):
    single, double = [], []
    for h in range(2):
        v = h * ONE
        gathers = not (last and h == 1)
        single += [("slots", 2 * h, g) for g in range(len(TR_GROUPS))]
        single += [("onehot", v + x) for x in range(2) if gathers]
        single += [("slots", 2 * h + 1, g) for g in range(len(TR_GROUPS))]
        single += [("onehot", v + x) for x in range(2, ONE) if gathers]
        double += [("gram", t, u) for t in (2 * h, 2 * h + 1) for u in range(UNITS)]
        if h in PARTS[last]:
            first, tiles = PARTS[last][h]
            single += [("pairsT", first, k) for k in range(3)] + [("h2", first, m) for m in range(tiles // 2)]
            double += [("pairs", first, n) for n in range(PAIR_UNITS)] + [("h1", first, n) for n in range(2)]
    mailboxes = {f"bank{k}": single[k::BANKS] for k in range(BANKS)}
    return mailboxes | {f"banks{k}": double[k::2] for k in range(2)}


USES = {last: turns(last) for last in (False, True)}
MAILBOXES = list(USES[False])
MAILBOX_OF = {last: {use: m for m in MAILBOXES for use in USES[last][m]} for last in (False, True)}
START_USES = {m: len(range(int(m[-1]), ONE, BANKS)) if m.startswith("bank") and m[:5] != "banks" else 0
              for m in MAILBOXES}


def pair_base(g):
    return g * (g - 1) // 2


def unit_slots(n):
    slots = list(range(8 * n + 1, min(8 * n + 9, SLOTS)))
    half = len(slots) // 2
    return [(g, k if k < half else 4 + k - half) for k, g in enumerate(slots)]


def build(nc, dense, ids, ids_t, tables, w1, w2, b2, w3, y):
    f32, f32r, f16, i32 = mybir.dt.float32, mybir.dt.float32r, mybir.dt.float16, mybir.dt.int32
    ALU = mybir.AluOpType
    ACT = mybir.ActivationFunctionType

    dense_v = dense.rearrange("(p t) d -> p t d", t=TILES)
    ids_v = ids.rearrange("(p t) f -> p t f", t=TILES)

    ctx = ExitStack()
    with ctx:
        def sb(name, shape, dt=f32):
            return ctx.enter_context(nc.sbuf_tensor(name, shape, dt))

        def sem(name):
            return ctx.enter_context(nc.semaphore(name))

        emb = sb("emb", [P, BLOCK_TILES, TR_SLOTS, D])
        emb_t = sb("emb_t", [P, 2, P, STRIDE])
        staged = sb("staged", [P, 2, P, ONE])
        ids_sb = sb("ids_sb", [P, BLOCK_TILES, TABLES], i32)
        hi = sb("hi", [CHUNK_ROWS, ONE, CHUNKS, D], f32r)
        lo = sb("lo", [CHUNK_ROWS, ONE, CHUNKS, D], f32r)
        onehot = sb("onehot", [CHUNK_ROWS, ONEHOT_BUFFERS, HALF, PAIR], f32r)
        ids_f = sb("ids_f", [ONE, B], f16)
        pick = sb("pick", [ONE, ONE], f16)
        row_i = sb("row_i", [P, CHUNKS], i32)
        row_f = sb("row_f", [P, CHUNKS])
        ident = sb("ident", [P, P])
        gram = sb("gram", [P, BLOCK_TILES, QUADS, SIDE])
        pairs = sb("pairs", [P, SHARE, COLUMNS])
        top_in = sb("top_in", [P, 4, 2, BLOCK], f32r)
        w1_sb = [sb(f"w1_{part}", [P, 4, H1], f32r) for part in ("hi", "lo")]
        w2_sb = [sb(f"w2_{part}", [P, N1, H2], f32r) for part in ("hi", "lo")]
        w3_sb = sb("w3_sb", [P, H2])
        b2_sb = sb("b2_sb", [P, H2])
        h2 = sb("h2", [P, 2, H2])
        y_block = sb("y_block", [P, BLOCK_TILES])
        y_sb = sb("y_sb", [P, TILES])
        dense_in = [top_in[:, 0, a, :] for a in range(2)]
        pairs_in = [top_in[0:KP, 1:4, a, :] for a in range(2)]
        h1_in = [[top_in[:, k, a, :] for k in (1, 2, 0, 3)] for a in range(2)]
        emb_t_row = emb_t[:, :, :, :].rearrange("p a b c -> p (a b c)")
        raw = emb_t_row[0:CHUNK_ROWS, 0:ONE * CHUNKS * D].rearrange("p (k c d) -> p k c d", k=ONE, c=CHUNKS)
        ids_raw = emb_t_row[0:ONE, ONE * CHUNKS * D:ONE * CHUNKS * D + B].bitcast(i32)
        w2_raw = emb[:, 2, :, :].rearrange("p s d -> p (s d)")[:, 0:N1 * H2].rearrange("p (k n) -> p k n", k=N1)
        w1_raw = emb[:, 3, :, :].rearrange("p s d -> p (s d)")[:, 0:5 * H1].rearrange("p (k n) -> p k n", k=5)

        bank_ps = [ctx.enter_context(nc.psum_tensor(f"bank_ps{k}", [P, 4, P], f32)) for k in range(BANKS)]
        ids_ps = ctx.enter_context(nc.psum_tensor("ids_ps", [P, 2, PAIR], f32))
        gram_ps = [ctx.enter_context(nc.psum_tensor(f"gram_ps{k}", [P, GRAM_UNIT, P], f32)) for k in range(2)]

        ids_ready = [sem(f"ids_ready{i}") for i in range(BLOCK_TILES)]
        dense_ready = [sem(f"dense_ready{i}") for i in range(BLOCK_TILES)]
        gathered = [sem(f"gathered{i}") for i in range(BLOCK_TILES)]
        raw_ready = [sem(f"raw_ready{k}") for k in range(ONE)]
        ids_t_ready = sem("ids_t_ready")
        w1_ready = sem("w1_ready")
        w2_ready = sem("w2_ready")
        vectors_ready = sem("vectors_ready")
        hi_made = sem("hi_made")
        lo_made = sem("lo_made")
        ids_f_made = sem("ids_f_made")
        zeroed = sem("zeroed")
        consts_made = sem("consts_made")
        rows_made = sem("rows_made")
        pads_made = sem("pads_made")
        w1_summed = sem("w1_summed")
        w_hi_made = sem("w_hi_made")
        w_lo_made = sem("w_lo_made")
        dense_hi_made = sem("dense_hi_made")
        dense_lo_made = sem("dense_lo_made")
        pairs_hi_made = sem("pairs_hi_made")
        h1_hi_made = sem("h1_hi_made")
        ids_spread = sem("ids_spread")
        onehot_ready = sem("onehot_ready")
        onehot_used = sem("onehot_used")
        moved = sem("moved")
        h2_biased = sem("h2_biased")
        h2_folded = sem("h2_folded")
        y_ready = sem("y_ready")
        y_stored = sem("y_stored")
        gather_begun, spread_begun = sem("gather_begun"), sem("spread_begun")
        full = {m: sem(f"{m}_full") for m in MAILBOXES}
        taken = {m: sem(f"{m}_taken") for m in MAILBOXES}
        takers = {m: 2 if m.startswith("banks") else 1 for m in MAILBOXES}

        def wait_full(eng, at, use):
            b, last = at
            m = MAILBOX_OF[last][use]
            filled = [[x for x in USES[z][m] if x[0] != "onehot"] for z in (False, last)]
            eng.wait_ge(full[m], b * len(filled[0]) + (filled[1].index(use) + 1))

        def takes(at, use, more):
            b, last = at
            m = MAILBOX_OF[last][use]
            return b * (takers[m] * len(USES[False][m])) \
                + takers[m] * (START_USES[m] + USES[last][m].index(use) + more)

        def wait_empty(eng, at, use):
            eng.wait_ge(taken[MAILBOX_OF[at[1]][use]], takes(at, use, 1))

        def wait_taken(eng, at, use):
            eng.wait_ge(taken[MAILBOX_OF[at[1]][use]], takes(at, use, 2))

        def halves(at, v):
            return at[0] * (HALVES * UNITS_OH) + HALVES * (ONE + v)

        def bank(at, use):
            m = MAILBOX_OF[at[1]][use]
            return bank_ps[int(m[-1])], full[m], taken[m]

        def banks(at, use):
            m = MAILBOX_OF[at[1]][use]
            return gram_ps[int(m[-1])], full[m], taken[m]

        def row(ps):
            return ps.rearrange("n g c -> n (g c)")

        block = ctx.enter_context(nc.Block())

        def load_raw(eng, k):
            table = tables[ONEHOT_TABLES[k]].rearrange("(p c) d -> p c d", c=CHUNKS)
            for rows in (slice(0, 112), slice(112, CHUNK_ROWS)):
                eng.dma_start(raw[rows, k, :, :], table[rows, :, :]).then_inc(raw_ready[k], 16)

        @block.sync
        def _(sp):
            def load_tile(t, i):
                sp.dma_start(ids_sb[:, i:i + 1, :], ids_v[:, bass.ds(t, 1), :]).then_inc(ids_ready[i], 16)
                sp.dma_start(emb[:, i, 0:1, :], dense_v[:, bass.ds(t, 1), :]).then_inc(dense_ready[i], 16)

            load_tile(0, 0)
            for k in range(1, ONE, 2):
                load_raw(sp, k)
            load_tile(1, 1)
            sp.dma_start(w2_raw, w2.rearrange("(k p) n -> p k n", p=P)).then_inc(w2_ready, 16)
            sp.dma_start(w1_raw[:, 3, :], w1[0:D, :]).then_inc(w1_ready, 16)
            sp.dma_start(w1_raw[:, 4, :], w1[D + COLUMNS:D + COLUMNS + D, :]).then_inc(w1_ready, 16)
            sp.dma_start(w1_raw[0:KP, 0:3, :], w1[D:D + COLUMNS, :].rearrange("(k p) n -> p k n", p=KP))\
              .then_inc(w1_ready, 16)
            for i, parts in ((2, 1), (3, 3)):
                sp.wait_ge(w_hi_made, parts)
                sp.wait_ge(w_lo_made, parts)
                load_tile(i, i)
            with sp.Fori(1, BLOCKS) as b:
                for i in range(BLOCK_TILES):
                    wait_taken(sp, (b - 1, False), ("slots", i, len(TR_GROUPS) - 1))
                    load_tile(b * BLOCK_TILES + i, i)
            sp.wait_ge(y_ready, BLOCKS + 1)
            sp.dma_start(y.rearrange("(p t) o -> p (t o)", t=TILES), y_sb[:, :]).then_inc(y_stored, 16)
            sp.wait_ge(y_stored, 16)

        @block.gpsimd
        def _(pool):
            pool.memset(ident[:, :], 0.0).then_inc(zeroed, 1)
            pool.memset(pick[:, :], 0.0).then_inc(zeroed, 1)
            pool.iota(row_i[:, :], pattern=[[1, CHUNKS]], base=0, channel_multiplier=CHUNKS).then_inc(consts_made, 1)
            pool.wait_ge(zeroed, 2)
            pool.affine_select(out=ident[:, :], in_=ident[:, :], compare_op=ALU.not_equal, fill=1.0, base=0,
                               pattern=[[-1, P]], channel_multiplier=1).then_inc(consts_made, 1)
            pool.affine_select(out=pick[:, :], in_=pick[:, :], compare_op=ALU.not_equal, fill=1.0, base=0,
                               pattern=[[-1, ONE]], channel_multiplier=1).then_inc(consts_made, 1)
            with pool.Fori(0, BLOCKS) as b:
                for i in range(BLOCK_TILES):
                    pool.wait_ge(ids_ready[i], b * 16 + 16)
                    pool.sem_inc(gather_begun, 1)
                    for s, t in enumerate(GATHERED):
                        pool.indirect_dma_start(
                            emb[:, i, 1 + s, :], None, tables[t],
                            bass.IndirectOffsetOnAxis(ap=ids_sb[:, i, t:t + 1], axis=0),
                        ).then_inc(gathered[i], 16)

        @block.scalar
        def _(act):
            act.dma_start(ids_raw, ids_t).then_inc(ids_t_ready, 16)
            for k in range(0, ONE, 2):
                load_raw(act, k)
            act.dma_start(b2_sb[:, :], b2.rearrange("(a n) -> a n", a=1).to_broadcast([P, H2])).then_inc(vectors_ready, 16)
            act.dma_start(w3_sb[:, :], w3.rearrange("(a n) o -> a (n o)", a=1).to_broadcast([P, H2]))\
               .then_inc(vectors_ready, 16)
            for k in range(ONE):
                act.wait_ge(raw_ready[k], 32)
                act.activation(hi[:, k, :, :], raw[:, k, :, :], ACT.Copy).then_inc(hi_made, 1)

            def stage(ps, u, free):
                act.activation(staged[:, :, :, u], ps[:, 0:2, :], ACT.Copy).then_inc(free, 1)

            for u in range(ONE):
                act.wait_ge(onehot_used, HALVES * (u + 1))
                stage(bank_ps[u % BANKS], u, taken[f"bank{u % BANKS}"])
            act.wait_ge(w2_ready, 16)
            act.activation(w2_sb[0][:, :, :], w2_raw, ACT.Copy).then_inc(w_hi_made, 1)
            act.wait_ge(w1_ready, 3 * 16)
            act.activation(w1_sb[0][0:KP, 0:3, :], w1_raw[0:KP, 0:3, :], ACT.Copy).then_inc(w_hi_made, 1)
            act.wait_ge(w1_summed, 1)
            act.activation(w1_sb[0][:, 3, :], w1_raw[:, 3, :], ACT.Copy).then_inc(w_hi_made, 1)
            act.wait_ge(pads_made, 3)

            def run_block(at):
                def take_onehot(v):
                    ps, _, free = bank(at, ("onehot", v))
                    act.wait_ge(onehot_used, halves(at, v + 1))
                    stage(ps, v % ONE, free)

                def move_staged(i):
                    act.activation(emb_t[:, i % 2, :, TR_SLOTS:SLOTS], staged[:, i % 2, :, :], ACT.Copy)\
                       .then_inc(moved, 1)

                def take_slots(i):
                    for g, slots in enumerate(TR_GROUPS):
                        use = ("slots", i, g)
                        ps, _, free = bank(at, use)
                        wait_full(act, at, use)
                        if g == 0:
                            act.activation(dense_in[0][:, i * P:(i + 1) * P], ps[:, 0, :], ACT.Copy)\
                               .then_inc(dense_hi_made, 1)
                        n = len(slots)
                        act.activation(emb_t[:, i % 2, :, slots[0]:slots[0] + n],
                                       ps[:, 0:n, :].rearrange("d f p -> d p f"), ACT.Copy).then_inc(free, 1)

                def take_gram(i, u):
                    use = ("gram", i, u)
                    ps, _, free = banks(at, use)
                    wait_full(act, at, use)
                    for j in (0, 1):
                        last = act.activation(
                            gram[STRIDE * j:STRIDE * j + SIDE, i, u * GRAM_UNIT:(u + 1) * GRAM_UNIT, :],
                            ps[STRIDE * j:STRIDE * j + SIDE, :, j * SIDE:(j + 1) * SIDE], ACT.Copy)
                    last.then_inc(free, 1)

                def take_pairs(first, tiles):
                    lanes = tiles * QUADS
                    for n in range(PAIR_UNITS):
                        use = ("pairs", first, n)
                        ps, _, free = banks(at, use)
                        wait_full(act, at, use)
                        for g, place in (x for x in unit_slots(n) if x[1] < 4):
                            last = act.activation(
                                pairs[0:lanes, :, pair_base(g):pair_base(g + 1)],
                                ps[0:lanes, place, :].rearrange("q (j f) -> q j f", j=SHARE)[:, :, 0:g], ACT.Copy)
                        last.then_inc(free, 1)

                def split_first_in(first, tiles):
                    lanes = tiles * QUADS
                    for k in range(3):
                        use = ("pairsT", first, k)
                        ps, _, _ = bank(at, use)
                        wait_full(act, at, use)
                        act.activation(pairs_in[0][:, k, 0:tiles * P].rearrange("k (q j) -> k q j", j=SHARE),
                                       ps[0:KP, :, 0:lanes].rearrange("k j q -> k q j"), ACT.Copy)\
                           .then_inc(pairs_hi_made, 1)

                def first_relu(first, tiles):
                    for n in range(2):
                        use = ("h1", first, n)
                        ps, _, _ = banks(at, use)
                        wait_full(act, at, use)
                        for k in range(2):
                            act.activation(h1_in[0][2 * n + k][:, 0:tiles * P],
                                           row(ps[:, 4 * k:4 * k + 4, :])[:, 0:tiles * P], ACT.Relu)\
                               .then_inc(h1_hi_made, 1)

                for h in range(2):
                    i, v = 2 * h, h * ONE
                    more = not (at[1] and h == 1)
                    top = h in PARTS[at[1]]
                    take_slots(i)
                    wait_taken(act, at, ("slots", i, len(TR_GROUPS) - 1))
                    move_staged(i)
                    move_staged(i + 1)
                    if more:
                        act.wait_ge(moved, at[0] * BLOCK_TILES + (i + 2))
                        take_onehot(v)
                    take_gram(i, 0)
                    take_gram(i, 1)
                    if more:
                        take_onehot(v + 1)
                    take_gram(i, 2)
                    take_slots(i + 1)
                    take_gram(i, 3)
                    beside = BESIDE[h] if more else 0
                    for u in range(UNITS):
                        if u < beside:
                            take_onehot(v + 2 + u)
                        take_gram(i + 1, u)
                    if top and not at[1]:
                        take_onehot(v + ONE - 2)
                    if top:
                        take_pairs(*PARTS[at[1]][h])
                        if not at[1]:
                            take_onehot(v + ONE - 1)
                        split_first_in(*PARTS[at[1]][h])
                        first_relu(*PARTS[at[1]][h])

            with act.Fori(0, BLOCKS - 1) as b:
                run_block((b, False))
            run_block((BLOCKS - 1, True))

        @block.vector
        def _(dve):
            dve.wait_ge(ids_t_ready, 16)
            dve.tensor_copy(ids_f[:, :], ids_raw).then_inc(ids_f_made, 1)
            dve.wait_ge(ids_f_made, 1)
            dve.memset(gram[:, :, :, :], 0.0).then_inc(pads_made, 1)
            dve.wait_ge(consts_made, 3)
            dve.tensor_copy(row_f[:, :], row_i[:, :]).then_inc(rows_made, 1)
            dve.wait_ge(rows_made, 1)

            def make_onehot(k, s, n):
                dve.tensor_tensor(
                    onehot[:, n % ONEHOT_BUFFERS, :, :],
                    ids_ps[0:CHUNK_ROWS, k, :].unsqueeze(1).to_broadcast([CHUNK_ROWS, HALF, PAIR]),
                    row_f[0:CHUNK_ROWS, s * HALF:(s + 1) * HALF].unsqueeze(2)
                    .to_broadcast([CHUNK_ROWS, HALF, PAIR]),
                    ALU.is_equal).then_inc(onehot_ready, 1)

            for u in range(ONE):
                dve.wait_ge(hi_made, u + 1)
                dve.tensor_tensor(lo[:, u, :, :], raw[:, u, :, :], hi[:, u, :, :].bitcast(f32), ALU.subtract)\
                   .then_inc(lo_made, 1)
                dve.wait_ge(ids_spread, u // 2 + 1)
                for s in range(HALVES):
                    n = HALVES * u + s
                    if n >= ONEHOT_BUFFERS:
                        dve.wait_ge(onehot_used, n + 1 - ONEHOT_BUFFERS)
                    make_onehot(u % 2, s, n)
            dve.wait_ge(lo_made, ONE)
            dve.memset(emb_t[:, :, :, SLOTS:STRIDE], 0.0).then_inc(pads_made, 1)
            dve.memset(pairs[:, :, PAIRS:PAIRS + 1], 1.0)
            dve.memset(pairs[:, :, PAIRS + 1:COLUMNS], 0.0).then_inc(pads_made, 1)

            def next_onehot(at, v, s):
                if v >= (ONE if at[1] else UNITS_OH + 2):
                    return
                if v % 2 == 0 and s == 0:
                    dve.wait_ge(ids_spread, at[0] * FILLS + (START_FILLS + v // 2))
                dve.wait_ge(onehot_used, halves(at, v) + (s + 1 - ONEHOT_BUFFERS))
                make_onehot(v % 2, s, HALVES * (ONE + v) + s)

            next_onehot((0, False), 0, 0)
            next_onehot((0, False), 0, 1)
            next_onehot((0, False), 1, 0)
            dve.wait_ge(w_hi_made, 1)
            dve.tensor_tensor(w2_sb[1][:, :, :], w2_raw, w2_sb[0][:, :, :].bitcast(f32), ALU.subtract)\
               .then_inc(w_lo_made, 1)
            dve.wait_ge(w1_ready, 3 * 16)
            dve.tensor_tensor(w1_raw[:, 3, :], w1_raw[:, 3, :], w1_raw[:, 4, :], ALU.add).then_inc(w1_summed, 1)
            dve.wait_ge(w_hi_made, 2)
            dve.tensor_tensor(w1_sb[1][0:KP, 0:3, :], w1_raw[0:KP, 0:3, :], w1_sb[0][0:KP, 0:3, :].bitcast(f32),
                              ALU.subtract).then_inc(w_lo_made, 1)
            dve.wait_ge(w_hi_made, 3)
            dve.wait_ge(w1_summed, 1)
            dve.tensor_tensor(w1_sb[1][:, 3, :], w1_raw[:, 3, :], w1_sb[0][:, 3, :].bitcast(f32), ALU.subtract)\
               .then_inc(w_lo_made, 1)
            dve.wait_ge(vectors_ready, 2 * 16)

            def run_block(at):
                def take_gram(i, u):
                    use = ("gram", i, u)
                    ps, _, free = banks(at, use)
                    wait_full(dve, at, use)
                    for j in (2, 3):
                        last = dve.tensor_copy(
                            gram[STRIDE * j:STRIDE * j + SIDE, i, u * GRAM_UNIT:(u + 1) * GRAM_UNIT, :],
                            ps[STRIDE * j:STRIDE * j + SIDE, :, j * SIDE:(j + 1) * SIDE])
                    last.then_inc(free, 1)

                def split_dense(i):
                    dve.wait_ge(dense_hi_made, at[0] * BLOCK_TILES + (i + 1))
                    wait_taken(dve, at, ("slots", i, 0))
                    dve.tensor_tensor(dense_in[1][:, i * P:(i + 1) * P], emb_t[:, i % 2, :, 0],
                                      dense_in[0][:, i * P:(i + 1) * P].bitcast(f32), ALU.subtract)\
                       .then_inc(dense_lo_made, 1)

                def take_pairs(first, tiles):
                    lanes = tiles * QUADS
                    for n in range(PAIR_UNITS):
                        use = ("pairs", first, n)
                        ps, _, free = banks(at, use)
                        wait_full(dve, at, use)
                        for g, place in (x for x in unit_slots(n) if x[1] >= 4):
                            last = dve.tensor_copy(
                                pairs[0:lanes, :, pair_base(g):pair_base(g + 1)],
                                ps[0:lanes, place, :].rearrange("q (j f) -> q j f", j=SHARE)[:, :, 0:g])
                        last.then_inc(free, 1)

                def split_first_in(first, tiles):
                    lanes = tiles * QUADS
                    for k in range(3):
                        ps, _, free = bank(at, ("pairsT", first, k))
                        dve.wait_ge(pairs_hi_made, at[0] * 3 + (3 * (first // 2 if at[1] else 0) + k + 1))
                        hi_part, lo_part = (pairs_in[a][:, k, 0:tiles * P].rearrange("k (q j) -> k q j", j=SHARE)
                                            for a in range(2))
                        dve.tensor_tensor(lo_part, ps[0:KP, :, 0:lanes].rearrange("k j q -> k q j"),
                                          hi_part.bitcast(f32), ALU.subtract).then_inc(free, 1)

                def first_relu(first, tiles):
                    for n in range(2):
                        ps, _, free = banks(at, ("h1", first, n))
                        for k in range(2):
                            dve.wait_ge(h1_hi_made, at[0] * 4 + (4 * (first // 2 if at[1] else 0) + 2 * n + k + 1))
                            last = dve.scalar_tensor_tensor(
                                h1_in[1][2 * n + k][:, 0:tiles * P], row(ps[:, 4 * k:4 * k + 4, :])[:, 0:tiles * P],
                                0.0, h1_in[0][2 * n + k][:, 0:tiles * P].bitcast(f32), ALU.max, ALU.subtract)
                        last.then_inc(free, 2)

                def last_layers(first, tiles):
                    for m in range(tiles // 2):
                        use = ("h2", first, m)
                        ps, _, free = bank(at, use)
                        wait_full(dve, at, use)
                        dve.wait_ge(h2_folded, at[0] * BLOCK_TILES + (first + 2 * m + 1))
                        dve.tensor_tensor(h2[:, :, :], ps[:, :, :].rearrange("p (t a) c -> p t (a c)", t=2),
                                          b2_sb[:, :].unsqueeze(1).to_broadcast([P, 2, H2]), ALU.add).then_inc(free, 1)
                        wait_taken(dve, at, use)
                        for k in range(2):
                            tile = first + 2 * m + k
                            dve.scalar_tensor_tensor(h2[:, k, :], h2[:, k, :], 0.0, w3_sb[:, :], ALU.max, ALU.mult,
                                                     accum_out=y_block[:, tile:tile + 1]).then_inc(h2_folded, 1)
                    dve.wait_ge(h2_folded, at[0] * BLOCK_TILES + (first + tiles + 1))
                    dve.tensor_copy(y_sb[:, bass.ds(at[0] * BLOCK_TILES + first, tiles)],
                                    y_block[:, first:first + tiles]).then_inc(y_ready, 1)

                for h in range(2):
                    i, v = 2 * h, h * ONE
                    more = not (at[1] and h == 1)
                    top = h in PARTS[at[1]]

                    def make(*which):
                        for x, s in which:
                            if more:
                                next_onehot(at, v + x, s)

                    split_dense(i)
                    make((1, 1))
                    take_gram(i, 0)
                    make((2, 0))
                    take_gram(i, 1)
                    make((2, 1), (3, 0))
                    take_gram(i, 2)
                    split_dense(i + 1)
                    take_gram(i, 3)
                    make((3, 1))
                    take_gram(i + 1, 0)
                    make((4, 0), (4, 1))
                    if h == 0:
                        make((5, 0))
                        take_gram(i + 1, 1)
                        make((5, 1))
                        take_gram(i + 1, 2)
                        make((6, 0), (6, 1))
                        take_gram(i + 1, 3)
                        make((7, 0))
                    else:
                        take_gram(i + 1, 1)
                        make((5, 0))
                        take_gram(i + 1, 2)
                        take_gram(i + 1, 3)
                        make((5, 1))
                    if top:
                        part = PARTS[at[1]][h]
                        ordinary = not at[1]
                        take_pairs(*part)
                        if ordinary:
                            make((6, 0))
                        split_first_in(*part)
                        if ordinary:
                            make((6, 1), (7, 0))
                        first_relu(*part)
                        last_layers(*part)

            dve.sem_inc(h2_folded, 1)
            with dve.Fori(0, BLOCKS - 1) as b:
                run_block((b, False))
            run_block((BLOCKS - 1, True))

        @block.tensor
        def _(pe):
            for m in MAILBOXES:
                pe.sem_inc(taken[m], takers[m])
            pe.wait_ge(consts_made, 3)
            pe.wait_ge(ids_f_made, 1)

            def spread(k, table, pair):
                return pe.matmul(ids_ps[:, k, :], pick[:, table:table + 1].to_broadcast([ONE, P]), ids_f[:, bass.ds(pair * PAIR, PAIR)],
                                 start=True, stop=True)

            def multiply(ps, u, n):
                for s in range(HALVES):
                    for c in range(HALF):
                        for part in (hi, lo):
                            chunk = s * HALF + c
                            last = pe.matmul(row(ps[:, 0:2, :]), part[:, u, chunk, :],
                                             onehot[:, (n + s) % ONEHOT_BUFFERS, c, :],
                                             start=chunk == 0 and part is hi, stop=chunk == CHUNKS - 1 and part is lo)
                    last.then_inc(onehot_used, 1)
                    if s == 0:
                        yield

            for u in range(ONE):
                if u == 0:
                    spread(0, 0, 0)
                    spread(1, 1, 0).then_inc(ids_spread, 1)
                elif u % 2 and u + 1 < ONE:
                    pe.wait_ge(onehot_ready, HALVES * (u + 1))
                    for k in range(2):
                        if u + 1 + k < ONE:
                            last = spread(k, u + 1 + k, 0)
                    last.then_inc(ids_spread, 1)
                pe.wait_ge(lo_made, u + 1)
                pe.wait_ge(taken[f"bank{u % BANKS}"], u // BANKS + 1)
                pe.wait_ge(onehot_ready, HALVES * u + 1)
                for _ in multiply(bank_ps[u % BANKS], u, HALVES * u):
                    pe.wait_ge(onehot_ready, HALVES * u + 2)
            pe.wait_ge(onehot_ready, HALVES * ONE)
            spread(0, 0, 1)
            spread(1, 1, 1).then_inc(ids_spread, 1)
            pe.wait_ge(pads_made, 3)

            def run_block(at):
                b, is_last = at

                def next_ids(v):
                    pe.wait_ge(onehot_ready, halves(at, v))
                    pe.sem_inc(spread_begun, 1)
                    for k in range(2):
                        if not is_last or v + k < ONE:
                            last = spread(k, (v + k) % ONE, b * 2 + (1 + (v + k) // ONE))
                    last.then_inc(ids_spread, 1)

                def onehot_gather(v):
                    use = ("onehot", v)
                    wait_empty(pe, at, use)
                    pe.wait_ge(onehot_ready, halves(at, v) + 1)
                    for _ in multiply(bank(at, use)[0], v % ONE, HALVES * (ONE + v)):
                        pe.wait_ge(onehot_ready, halves(at, v) + 2)

                def transpose_tile(i):
                    pe.wait_ge(gathered[i], b * (16 * GATH) + 16 * GATH)
                    pe.wait_ge(dense_ready[i], b * 16 + 16)
                    for g, slots in enumerate(TR_GROUPS):
                        use = ("slots", i, g)
                        ps, ready, _ = bank(at, use)
                        wait_empty(pe, at, use)
                        for s in slots:
                            last = pe.transpose(ps[:, s - slots[0], :], emb[:, i, s, :], ident[:, :])
                        last.then_inc(ready, 1)

                def gram_products(i, u):
                    use = ("gram", i, u)
                    ps, ready, _ = banks(at, use)
                    if u == 0:
                        for g in range(len(TR_GROUPS))[-BANKS:]:
                            wait_taken(pe, at, ("slots", i, g))
                        pe.wait_ge(moved, b * BLOCK_TILES + i + 1)
                    wait_empty(pe, at, use)
                    for k in range(GRAM_UNIT):
                        first = (u * GRAM_UNIT + k) * SHARE
                        quad = emb_t[:, i % 2, first:first + SHARE, :]
                        last = pe.matmul(ps[0:ROWS, k, 0:SHARE * SIDE], quad.rearrange("d j f -> d (j f)")[:, 0:ROWS],
                                         quad[:, :, 1:SLOTS], start=True, stop=True)
                    last.then_inc(ready, 1)

                def turn_products(first, tiles):
                    for u in (UNITS - 2, UNITS - 1):
                        wait_taken(pe, at, ("gram", first + tiles - 1, u))
                    for n in range(PAIR_UNITS):
                        use = ("pairs", first, n)
                        ps, ready, _ = banks(at, use)
                        wait_empty(pe, at, use)
                        for g, place in unit_slots(n):
                            last = pe.transpose(
                                ps[0:tiles * QUADS, place, :],
                                gram[:, first:first + tiles, :, g - 1].rearrange("f t q -> f (t q)"), ident[:, :])
                        last.then_inc(ready, 1)

                def turn_pairs(first, tiles):
                    lanes = tiles * QUADS
                    for n in (PAIR_UNITS - 2, PAIR_UNITS - 1):
                        wait_taken(pe, at, ("pairs", first, n))
                    for k in range(3):
                        use = ("pairsT", first, k)
                        ps, ready, _ = bank(at, use)
                        wait_empty(pe, at, use)
                        for j in range(SHARE):
                            last = pe.transpose(ps[0:KP, j, 0:lanes], pairs[0:lanes, j, k * KP:(k + 1) * KP],
                                                ident[0:lanes, 0:lanes])
                        last.then_inc(ready, 1)

                def first_layer(first, tiles):
                    cols = tiles * P
                    out = [row(banks(at, ("h1", first, n // 2))[0][:, 4 * (n % 2):4 * (n % 2) + 4, :])[:, 0:cols]
                           for n in range(N1)]
                    pe.wait_ge(w_lo_made, 3)
                    pe.wait_ge(dense_lo_made, b * BLOCK_TILES + (first + tiles))
                    for n in range(N1):
                        for w, x in SPLIT_PRODUCTS:
                            pe.matmul(out[n], w1_sb[w][:, 3, n * P:(n + 1) * P], dense_in[x][:, first * P:first * P + cols],
                                      start=(w, x) == (0, 0), stop=False)
                    for k in range(3):
                        wait_taken(pe, at, ("pairsT", first, k))
                        for n in range(N1):
                            for w, x in SPLIT_PRODUCTS:
                                last = pe.matmul(out[n], w1_sb[w][0:KP, k, n * P:(n + 1) * P],
                                                 pairs_in[x][:, k, 0:cols],
                                                 start=False, stop=k == 2 and (w, x) == SPLIT_PRODUCTS[-1])
                            if k == 2 and n % 2:
                                last.then_inc(banks(at, ("h1", first, n // 2))[1], 1)

                def second_layer(first, tiles):
                    for m in range(tiles // 2):
                        wait_empty(pe, at, ("h2", first, m))
                    for t in range(2):
                        for half in range(2):
                            if t == 0:
                                wait_taken(pe, at, ("h1", first, half))
                            for m in range(tiles // 2):
                                ps, ready, _ = bank(at, ("h2", first, m))
                                s = (2 * m + t) * P
                                for k in (2 * half, 2 * half + 1):
                                    for w, x in SPLIT_PRODUCTS:
                                        last = pe.matmul(row(ps[:, 2 * t:2 * t + 2, :]), h1_in[x][k][:, s:s + P],
                                                         w2_sb[w][:, k, :], start=k == 0 and (w, x) == (0, 0),
                                                         stop=k == N1 - 1 and (w, x) == SPLIT_PRODUCTS[-1])
                                if t == 1 and half == 1:
                                    last.then_inc(ready, 1)

                for h in range(2):
                    i, v = 2 * h, h * ONE
                    more = not (is_last and h == 1)
                    top = h in PARTS[is_last]
                    transpose_tile(i)
                    if more:
                        onehot_gather(v)
                    gram_products(i, 0)
                    if more:
                        next_ids(v + 2)
                    gram_products(i, 1)
                    if more:
                        onehot_gather(v + 1)
                    gram_products(i, 2)
                    transpose_tile(i + 1)
                    gram_products(i, 3)
                    beside = BESIDE[h] if more else 0
                    for u in range(UNITS):
                        if u == 1 and more:
                            next_ids(v + 4)
                        if u == 3 and h == 0 and not is_last:
                            next_ids(v + 6)
                        if u < beside:
                            onehot_gather(v + 2 + u)
                        gram_products(i + 1, u)
                    if top and not is_last:
                        onehot_gather(v + ONE - 2)
                    if top:
                        turn_products(*PARTS[is_last][h])
                        if not is_last:
                            next_ids(UNITS_OH)
                            onehot_gather(v + ONE - 1)
                        turn_pairs(*PARTS[is_last][h])
                        first_layer(*PARTS[is_last][h])
                        second_layer(*PARTS[is_last][h])

            with pe.Fori(0, BLOCKS - 1) as b:
                run_block((b, False))
            run_block((BLOCKS - 1, True))


def kernel(**inputs):
    import concourse.bacc as bacc
    from concourse.bass_utils import run_bass_kernel_spmd

    nc = bacc.Bacc("TRN2", target_bir_lowering=False, num_devices=1)
    arrays = {}

    def give(name, a):
        a = np.ascontiguousarray(a)
        arrays[name] = a
        return nc.dram_tensor(name, a.shape, mybir.dt.from_np(a.dtype), kind="ExternalInput").ap()

    ids = np.asarray(inputs["ids"])
    w1 = np.asarray(inputs["W_top1"])
    slot_feature = [0] + [1 + t for t in SLOT_TABLES]
    order = []
    for g in range(1, SLOTS):
        for f in range(g):
            i, j = sorted((slot_feature[f], slot_feature[g]))
            order.append(D + i * SLOTS - i * (i + 1) // 2 + j - i - 1)
    w1 = np.concatenate([w1[:D], w1[order], np.asarray(inputs["b_top1"])[None],
                         np.zeros((COLUMNS - PAIRS - 1, H1), w1.dtype), w1[D + PAIRS:]])
    ids_t = ids[:, ONEHOT_TABLES].reshape(P, TILES, ONE).transpose(2, 1, 0).reshape(ONE, B)
    args = [give("dense", inputs["r_dense_output"]), give("ids", ids), give("ids_t", ids_t)]
    args.append([give(f"table{t}", inputs[f"tbl_{t}"]) for t in range(TABLES)])
    args += [give("w1", w1), give("w2", inputs["W_top2"]),
             give("b2", inputs["b_top2"]), give("w3", inputs["W_top3"])]
    y = nc.dram_tensor("y", (B, 1), mybir.dt.float32, kind="ExternalOutput").ap()
    build(nc, *args, y)
    r = run_bass_kernel_spmd(nc, [arrays], core_ids=[0])
    return r.results[0]["y"]
```

```python
from contextlib import ExitStack

import concourse.bass as bass
import numpy as np
from concourse import mybir

P = 128
B, D = 2048, 128
TABLES = 26
SLOTS = TABLES + 1
TILES = B // P
BLOCK_TILES = 4
BLOCKS = TILES // BLOCK_TILES
BLOCK = BLOCK_TILES * P
PAIR = 2 * P

ONEHOT_TABLES = [3, 5, 6, 7, 8, 11, 15]
GATHERED = [t for t in range(TABLES) if t not in ONEHOT_TABLES]
ONE, GATH = len(ONEHOT_TABLES), len(GATHERED)
SLOT_TABLES = GATHERED + ONEHOT_TABLES
VOCAB = 1000
CHUNKS = 8
CHUNK_ROWS = VOCAB // CHUNKS
HALF = CHUNKS // 2
HALVES = 2
ONEHOT_BUFFERS = 3
UNITS_OH = 2 * ONE
FILLS = UNITS_OH // 2
START_FILLS = (ONE + 1) // 2 + 1
HALF_BUFFER = [n % ONEHOT_BUFFERS for n in range(HALVES * UNITS_OH - 1)] + [1]
assert ONE == 7 and ONEHOT_BUFFERS == 3, "the order of the steps below counts on it"


def half_buffer(n):
    return HALF_BUFFER[n % len(HALF_BUFFER)]


def since_reuse(n):
    return next(d for d in range(1, len(HALF_BUFFER)) if half_buffer(n - d) == half_buffer(n))


TR_SLOTS = 1 + GATH
TR_GROUPS = [range(s, min(s + 4, TR_SLOTS)) for s in range(0, TR_SLOTS, 4)]
LATE = TR_GROUPS[-1][0]

SHARE = 4
SIDE = SLOTS - 1
ROWS = SLOTS * SHARE - 1
COPIES = [(j, SLOTS * j // 64 * 64, SLOTS * j + SIDE) for j in reversed(range(SHARE))]
QUADS = P // SHARE
GRAM_UNIT = 8
UNITS = QUADS // GRAM_UNIT
COPY_WAITS = (SHARE - 1) * UNITS * BLOCK_TILES
PAIRS = SLOTS * (SLOTS - 1) // 2
COLUMNS = -(-(PAIRS + 1) // 3) * 3
KP = COLUMNS // 3
H1, H2 = 512, 256
N1 = H1 // P

PARTS = {False: {1: (0, BLOCK_TILES)}, True: {0: (0, 2), 1: (2, 2)}}
PAIR_UNITS = 4
SPLIT_PRODUCTS = [(0, 0), (1, 0), (0, 1)]

BANKS = 3


def turns(last):
    single, double = [], []
    for h in range(2):
        v = h * ONE
        gathers = not (last and h == 1)
        single += [("slots", 2 * h, g) for g in range(len(TR_GROUPS))]
        single += [("onehot", v + x) for x in range(3) if gathers]
        single += [("slots", 2 * h + 1, g) for g in range(len(TR_GROUPS))]
        top = h in PARTS[last]
        single += [("onehot", v + x) for x in range(3, ONE - 1 if top else ONE) if gathers]
        double += [("gram", t, u) for t in (2 * h, 2 * h + 1) for u in range(UNITS)]
        if top:
            first, tiles = PARTS[last][h]
            single += [("pairsT", first, k) for k in range(3)]
            single += [("onehot", v + ONE - 1)] if gathers else []
            single += [("h2", first, m) for m in range(tiles // 2)]
            double += [("pairs", first, n) for n in range(PAIR_UNITS)] + [("h1", first, n) for n in range(2)]
    mailboxes = {f"bank{k}": single[k::BANKS] for k in range(BANKS)}
    return mailboxes | {f"banks{k}": double[k::2] for k in range(2)}


USES = {last: turns(last) for last in (False, True)}
MAILBOXES = list(USES[False])
MAILBOX_OF = {last: {use: m for m in MAILBOXES for use in USES[last][m]} for last in (False, True)}
START_USES = {m: len(range(int(m[-1]), ONE, BANKS)) if m.startswith("bank") and m[:5] != "banks" else 0
              for m in MAILBOXES}


def pair_base(g):
    return g * (g - 1) // 2


def unit_slots(n):
    slots = list(range(8 * n + 1, min(8 * n + 9, SLOTS)))
    half = len(slots) // 2
    return [(g, k if k < half else 4 + k - half) for k, g in enumerate(slots)]


def build(nc, dense, ids, ids_t, tables, w1, w2, b2, w3, y):
    f32, f32r, f16, i32 = mybir.dt.float32, mybir.dt.float32r, mybir.dt.float16, mybir.dt.int32
    ALU = mybir.AluOpType
    ACT = mybir.ActivationFunctionType

    dense_v = dense.rearrange("(p t) d -> p t d", t=TILES)
    ids_v = ids.rearrange("(p t) f -> p t f", t=TILES)

    ctx = ExitStack()
    with ctx:
        def sb(name, shape, dt=f32):
            return ctx.enter_context(nc.sbuf_tensor(name, shape, dt))

        def sem(name):
            return ctx.enter_context(nc.semaphore(name))

        emb = sb("emb", [P, BLOCK_TILES, TR_SLOTS, D])
        emb_t = sb("emb_t", [P, 2, P, SLOTS])
        staged = sb("staged", [P, 2, P, ONE])
        ids_sb = sb("ids_sb", [P, BLOCK_TILES, TABLES], i32)
        hi = sb("hi", [CHUNK_ROWS, ONE, CHUNKS, D], f32r)
        lo = sb("lo", [CHUNK_ROWS, ONE, CHUNKS, D], f32r)
        onehot = sb("onehot", [CHUNK_ROWS, ONEHOT_BUFFERS, HALF, PAIR], f32r)
        ids_f = sb("ids_f", [ONE, B], f16)
        pick = sb("pick", [ONE, ONE], f16)
        row_i = sb("row_i", [P, CHUNKS], i32)
        row_f = sb("row_f", [P, CHUNKS])
        ident = sb("ident", [P, P])
        gram = sb("gram", [P, BLOCK_TILES, QUADS, SIDE])
        pairs = sb("pairs", [P, SHARE, COLUMNS])
        top_in = sb("top_in", [P, 4, 2, BLOCK], f32r)
        w1_sb = [sb(f"w1_{part}", [P, 4, H1], f32r) for part in ("hi", "lo")]
        w2_sb = [sb(f"w2_{part}", [P, N1, H2], f32r) for part in ("hi", "lo")]
        w3_sb = sb("w3_sb", [P, H2])
        b2_sb = sb("b2_sb", [P, H2])
        y_block = sb("y_block", [P, BLOCK_TILES])
        y_sb = sb("y_sb", [P, TILES])
        dense_in = [top_in[:, 0, a, :] for a in range(2)]
        pairs_in = [top_in[0:KP, 1:4, a, :] for a in range(2)]
        h1_in = [[top_in[:, k, a, :] for k in (1, 2, 0, 3)] for a in range(2)]
        h2 = pairs[:, 0:BLOCK_TILES, 0:H2]
        emb_t_row = emb_t[:, :, :, :].rearrange("p a b c -> p (a b c)")
        in_emb_t = BLOCK_TILES // 2 * P * SLOTS // (CHUNKS * D)
        raw_rows = [emb_t_row[:, k * CHUNKS * D:(k + 1) * CHUNKS * D] for k in range(in_emb_t)]
        raw_rows.append(pairs[:, :, :].rearrange("p j n -> p (j n)")[:, 0:CHUNKS * D])
        raw = [rows[0:CHUNK_ROWS, :].rearrange("p (c d) -> p c d", c=CHUNKS) for rows in raw_rows]
        ids_raw = gram[0:ONE, :, :, :].bitcast(i32).rearrange("p t q g -> p (t q g)")[:, 0:B]
        w2_raw = gram[:, :, :, :].rearrange("p t q g -> p (t q g)")[:, B:B + N1 * H2].rearrange("p (k n) -> p k n", k=N1)
        w1_raw = emb[:, 3, :, :].rearrange("p s d -> p (s d)")[:, 0:5 * H1].rearrange("p (k n) -> p k n", k=5)

        bank_ps = [ctx.enter_context(nc.psum_tensor(f"bank_ps{k}", [P, 4, P], f32)) for k in range(BANKS)]
        ids_ps = ctx.enter_context(nc.psum_tensor("ids_ps", [P, 2, PAIR], f32))
        gram_ps = [ctx.enter_context(nc.psum_tensor(f"gram_ps{k}", [P, GRAM_UNIT, P], f32)) for k in range(2)]

        ids_ready = [sem(f"ids_ready{i}") for i in range(BLOCK_TILES)]
        dense_ready = [sem(f"dense_ready{i}") for i in range(BLOCK_TILES)]
        gathered = [[sem(f"gathered{i}_{part}") for part in ("early", "late")] for i in range(BLOCK_TILES)]
        raw_ready = [sem(f"raw_ready{k}") for k in range(ONE)]
        ids_t_ready = sem("ids_t_ready")
        w1_ready = sem("w1_ready")
        w2_ready = sem("w2_ready")
        vectors_ready = sem("vectors_ready")
        hi_made = sem("hi_made")
        lo_made = sem("lo_made")
        ids_f_made = sem("ids_f_made")
        zeroed = sem("zeroed")
        consts_made = sem("consts_made")
        rows_made = sem("rows_made")
        columns_made = sem("columns_made")
        w1_summed = sem("w1_summed")
        act_copied = sem("act_copied")
        dve_copied = sem("dve_copied")
        w_hi_made = sem("w_hi_made")
        w_lo_made = sem("w_lo_made")
        dense_hi_made = sem("dense_hi_made")
        dense_lo_made = sem("dense_lo_made")
        pairs_hi_made = sem("pairs_hi_made")
        h1_hi_made = sem("h1_hi_made")
        ids_spread = sem("ids_spread")
        onehot_ready = sem("onehot_ready")
        onehot_used = sem("onehot_used")
        moved = sem("moved")
        h2_biased = sem("h2_biased")
        h2_folded = sem("h2_folded")
        y_ready = sem("y_ready")
        y_stored = sem("y_stored")
        gather_begun, spread_begun = sem("gather_begun"), sem("spread_begun")
        full = {m: sem(f"{m}_full") for m in MAILBOXES}
        taken = {m: sem(f"{m}_taken") for m in MAILBOXES}
        takers = {m: 2 if m.startswith("banks") else 1 for m in MAILBOXES}

        def wait_full(eng, at, use):
            b, last = at
            m = MAILBOX_OF[last][use]
            filled = [[x for x in USES[z][m] if x[0] != "onehot"] for z in (False, last)]
            eng.wait_ge(full[m], b * len(filled[0]) + (filled[1].index(use) + 1))

        def takes(at, use, more):
            b, last = at
            m = MAILBOX_OF[last][use]
            return b * (takers[m] * len(USES[False][m])) \
                + takers[m] * (START_USES[m] + USES[last][m].index(use) + more)

        def wait_empty(eng, at, use):
            eng.wait_ge(taken[MAILBOX_OF[at[1]][use]], takes(at, use, 1))

        def wait_taken(eng, at, use):
            eng.wait_ge(taken[MAILBOX_OF[at[1]][use]], takes(at, use, 2))

        def halves(at, v):
            return at[0] * (HALVES * UNITS_OH) + HALVES * (ONE + v)

        def bank(at, use):
            m = MAILBOX_OF[at[1]][use]
            return bank_ps[int(m[-1])], full[m], taken[m]

        def banks(at, use):
            m = MAILBOX_OF[at[1]][use]
            return gram_ps[int(m[-1])], full[m], taken[m]

        def row(ps):
            return ps.rearrange("n g c -> n (g c)")

        block = ctx.enter_context(nc.Block())

        def load_raw(eng, k):
            table = tables[ONEHOT_TABLES[k]].rearrange("(p c) d -> p c d", c=CHUNKS)
            for rows in (slice(0, 112), slice(112, CHUNK_ROWS)):
                eng.dma_start(raw[k][rows, :, :], table[rows, :, :]).then_inc(raw_ready[k], 16)

        @block.sync
        def _(sp):
            def load_tile(t, i):
                sp.dma_start(ids_sb[:, i:i + 1, :], ids_v[:, bass.ds(t, 1), :]).then_inc(ids_ready[i], 16)
                sp.dma_start(emb[:, i, 0:1, :], dense_v[:, bass.ds(t, 1), :]).then_inc(dense_ready[i], 16)

            load_tile(0, 0)
            for k in range(1, ONE):
                load_raw(sp, k)
            load_tile(1, 1)
            sp.dma_start(w2_raw, w2.rearrange("(k p) n -> p k n", p=P)).then_inc(w2_ready, 16)
            sp.dma_start(b2_sb[:, :], b2.rearrange("(a n) -> a n", a=1).to_broadcast([P, H2])).then_inc(vectors_ready, 16)
            sp.dma_start(w3_sb[:, :], w3.rearrange("(a n) o -> a (n o)", a=1).to_broadcast([P, H2]))\
              .then_inc(vectors_ready, 16)
            sp.dma_start(w1_raw[:, 3, :], w1[0:D, :]).then_inc(w1_ready, 16)
            sp.dma_start(w1_raw[:, 4, :], w1[D + COLUMNS:D + COLUMNS + D, :]).then_inc(w1_ready, 16)
            sp.dma_start(w1_raw[0:KP, 0:3, :], w1[D:D + COLUMNS, :].rearrange("(k p) n -> p k n", p=KP))\
              .then_inc(w1_ready, 16)
            load_tile(2, 2)
            sp.wait_ge(w_hi_made, 3)
            sp.wait_ge(w_lo_made, 3)
            load_tile(3, 3)
            with sp.Fori(1, BLOCKS) as b:
                for i in range(BLOCK_TILES):
                    wait_taken(sp, (b - 1, False), ("slots", i, len(TR_GROUPS) - 1))
                    load_tile(b * BLOCK_TILES + i, i)
            sp.wait_ge(y_ready, BLOCKS - 1 + len(PARTS[True]))
            sp.dma_start(y.rearrange("(p t) o -> p (t o)", t=TILES), y_sb[:, :]).then_inc(y_stored, 16)
            sp.wait_ge(y_stored, 16)

        @block.gpsimd
        def _(pool):
            pool.memset(ident[:, :], 0.0).then_inc(zeroed, 1)
            pool.memset(pick[:, :], 0.0).then_inc(zeroed, 1)
            pool.iota(row_i[:, :], pattern=[[1, CHUNKS]], base=0, channel_multiplier=CHUNKS).then_inc(consts_made, 1)
            pool.wait_ge(zeroed, 2)
            pool.affine_select(out=ident[:, :], in_=ident[:, :], compare_op=ALU.not_equal, fill=1.0, base=0,
                               pattern=[[-1, P]], channel_multiplier=1).then_inc(consts_made, 1)
            pool.affine_select(out=pick[:, :], in_=pick[:, :], compare_op=ALU.not_equal, fill=1.0, base=0,
                               pattern=[[-1, ONE]], channel_multiplier=1).then_inc(consts_made, 1)
            with pool.Fori(0, BLOCKS) as b:
                for i in range(BLOCK_TILES):
                    pool.wait_ge(ids_ready[i], b * 16 + 16)
                    pool.sem_inc(gather_begun, 1)
                    for s, t in enumerate(GATHERED):
                        pool.indirect_dma_start(
                            emb[:, i, 1 + s, :], None, tables[t],
                            bass.IndirectOffsetOnAxis(ap=ids_sb[:, i, t:t + 1], axis=0),
                        ).then_inc(gathered[i][1 + s >= LATE], 16)

        @block.scalar
        def _(act):
            act.dma_start(ids_raw, ids_t).then_inc(ids_t_ready, 16)
            load_raw(act, 0)
            for k in range(ONE):
                act.wait_ge(raw_ready[k], 32)
                act.activation(hi[:, k, :, :], raw[k], ACT.Copy).then_inc(hi_made, 1)

            def stage(ps, u, free):
                act.activation(staged[:, :, :, u], ps[:, 0:2, :], ACT.Copy).then_inc(free, 1)

            for u in range(ONE):
                act.wait_ge(onehot_used, HALVES * (u + 1))
                stage(bank_ps[u % BANKS], u, taken[f"bank{u % BANKS}"])
                if u == 3:
                    act.wait_ge(w2_ready, 16)
                    act.activation(w2_sb[0][:, :, :], w2_raw, ACT.Copy).then_inc(w_hi_made, 1)
                if u == 4:
                    act.wait_ge(w1_ready, 3 * 16)
                    act.activation(w1_sb[0][0:KP, 0:3, :], w1_raw[0:KP, 0:3, :], ACT.Copy).then_inc(w_hi_made, 1)
                if u == 5:
                    act.wait_ge(w1_summed, 1)
                    act.activation(w1_sb[0][:, 3, :], w1_raw[:, 3, :], ACT.Copy).then_inc(w_hi_made, 1)
            act.wait_ge(taken[f"bank{(ONE - 1) % BANKS}"], 1 + ONE // BANKS)
            act.wait_ge(columns_made, 1)

            def run_block(at):
                def take_onehot(v):
                    ps, _, free = bank(at, ("onehot", v))
                    act.wait_ge(onehot_used, halves(at, v + 1))
                    stage(ps, v % ONE, free)

                def move_staged(i):
                    act.activation(emb_t[:, i % 2, :, TR_SLOTS:SLOTS], staged[:, i % 2, :, :], ACT.Copy)\
                       .then_inc(moved, 1)

                def take_slots(i):
                    for g, slots in enumerate(TR_GROUPS):
                        use = ("slots", i, g)
                        ps, _, free = bank(at, use)
                        wait_full(act, at, use)
                        n = len(slots)
                        act.activation(emb_t[:, i % 2, :, slots[0]:slots[0] + n],
                                       ps[:, 0:n, :].rearrange("d f p -> d p f"), ACT.Copy).then_inc(free, 1)

                def take_gram(i, u):
                    use = ("gram", i, u)
                    ps, _, free = banks(at, use)
                    wait_full(act, at, use)
                    for n, (j, start, end) in enumerate(COPIES):
                        if n:
                            last.then_inc(act_copied, 1)
                            act.wait_ge(act_copied, at[0] * COPY_WAITS + ((i * UNITS + u) * (SHARE - 1) + n))
                        last = act.activation(gram[start:end, i, u * GRAM_UNIT:u * GRAM_UNIT + GRAM_UNIT // 2, :],
                                              ps[start:end, 0:GRAM_UNIT // 2, j * SIDE:(j + 1) * SIDE], ACT.Copy)
                    last.then_inc(free, 1)

                def take_pairs(first, tiles):
                    lanes = tiles * QUADS
                    for n in range(PAIR_UNITS):
                        use = ("pairs", first, n)
                        ps, _, free = banks(at, use)
                        wait_full(act, at, use)
                        for g, place in (x for x in unit_slots(n) if x[1] < 4):
                            last = act.activation(
                                pairs[0:lanes, :, pair_base(g):pair_base(g + 1)],
                                ps[0:lanes, place, 0:SHARE * SLOTS].rearrange("q (j f) -> q j f", j=SHARE)[:, :, 0:g], ACT.Copy)
                        last.then_inc(free, 1)

                def split_first_in(first, tiles):
                    lanes = tiles * QUADS
                    for k in range(3):
                        use = ("pairsT", first, k)
                        ps, _, _ = bank(at, use)
                        wait_full(act, at, use)
                        act.activation(pairs_in[0][:, k, 0:tiles * P].rearrange("k (q j) -> k q j", j=SHARE),
                                       ps[0:KP, :, 0:lanes].rearrange("k j q -> k q j"), ACT.Copy)\
                           .then_inc(pairs_hi_made, 1)

                def first_relu(first, tiles):
                    for n in range(2):
                        use = ("h1", first, n)
                        ps, _, _ = banks(at, use)
                        wait_full(act, at, use)
                        for k in range(2):
                            act.activation(h1_in[0][2 * n + k][:, 0:tiles * P],
                                           row(ps[:, 4 * k:4 * k + 4, :])[:, 0:tiles * P], ACT.Relu)\
                               .then_inc(h1_hi_made, 1)

                for h in range(2):
                    i, v = 2 * h, h * ONE
                    more = not (at[1] and h == 1)
                    top = h in PARTS[at[1]]
                    def gather(*units):
                        for x in units:
                            if more:
                                take_onehot(v + x)

                    def staged_all(u):
                        if u >= 0:
                            wait_taken(act, at, ("onehot", u))
                        else:
                            m = MAILBOX_OF[False]["onehot", UNITS_OH - 1]
                            uses = USES[False][m]
                            act.wait_ge(taken[m], at[0] * len(uses)
                                        + (START_USES[m] + uses.index(("onehot", UNITS_OH - 1)) + 2 - len(uses)))

                    if h == 0:
                        staged_all(-1)
                        move_staged(i)
                        move_staged(i + 1)
                    take_slots(i)
                    if h == 1:
                        if more:
                            staged_all(v - 1)
                            move_staged(i)
                        move_staged(i + 1)
                    if more:
                        act.wait_ge(moved, at[0] * BLOCK_TILES + (i + 2))
                    gather(0)
                    take_gram(i, 0)
                    take_gram(i, 1)
                    if not more:
                        take_slots(i + 1)
                    gather(1)
                    take_gram(i, 2)
                    take_gram(i, 3)
                    gather(2)
                    if more:
                        take_slots(i + 1)
                    gather(3)
                    take_gram(i + 1, 0)
                    take_gram(i + 1, 1)
                    if not top:
                        gather(4)
                        take_gram(i + 1, 2)
                        gather(5)
                        take_gram(i + 1, 3)
                        gather(6)
                    else:
                        part = PARTS[at[1]][h]
                        take_gram(i + 1, 2)
                        take_gram(i + 1, 3)
                        gather(4)
                        take_pairs(*part)
                        gather(5)
                        split_first_in(*part)
                        first_relu(*part)
                        gather(6)
                        if h == 0:
                            staged_all(v + 6)
                            move_staged(i + 2)

            with act.Fori(0, BLOCKS - 1) as b:
                run_block((b, False))
            run_block((BLOCKS - 1, True))

        @block.vector
        def _(dve):
            dve.wait_ge(ids_t_ready, 16)
            dve.tensor_copy(ids_f[:, :], ids_raw).then_inc(ids_f_made, 1)
            dve.wait_ge(ids_f_made, 1)
            dve.wait_ge(consts_made, 3)
            dve.tensor_copy(row_f[:, :], row_i[:, :]).then_inc(rows_made, 1)
            dve.wait_ge(rows_made, 1)

            def make_onehot(k, s, n):
                dve.tensor_tensor(
                    onehot[:, half_buffer(n), :, :],
                    ids_ps[0:CHUNK_ROWS, k, :].unsqueeze(1).to_broadcast([CHUNK_ROWS, HALF, PAIR]),
                    row_f[0:CHUNK_ROWS, s * HALF:(s + 1) * HALF].unsqueeze(2)
                    .to_broadcast([CHUNK_ROWS, HALF, PAIR]),
                    ALU.is_equal).then_inc(onehot_ready, 1)

            def first_onehot(n):
                u, s = n // HALVES, n % HALVES
                dve.wait_ge(ids_spread, u // 2 + 1)
                place = HALVES * (UNITS_OH - ONE) + n
                if n >= since_reuse(place):
                    dve.wait_ge(onehot_used, n + 1 - since_reuse(place))
                make_onehot(u % 2, s, place)

            def split_table(u):
                dve.wait_ge(hi_made, u + 1)
                dve.tensor_tensor(lo[:, u, :, :], raw[u], hi[:, u, :, :].bitcast(f32), ALU.subtract)\
                   .then_inc(lo_made, 1)

            for n in range(ONEHOT_BUFFERS):
                first_onehot(n)
            split_table(0)
            split_table(1)
            split_table(2)
            first_onehot(3)
            for u in range(2, ONE):
                if u + 1 < ONE:
                    split_table(u + 1)
                first_onehot(HALVES * u)
                first_onehot(HALVES * u + 1)
                if u == 4:
                    dve.wait_ge(w1_ready, 3 * 16)
                    dve.tensor_tensor(w1_raw[:, 3, :], w1_raw[:, 3, :], w1_raw[:, 4, :], ALU.add).then_inc(w1_summed, 1)
            dve.wait_ge(lo_made, ONE)
            dve.memset(pairs[:, :, PAIRS:PAIRS + 1], 1.0)
            dve.memset(pairs[:, :, PAIRS + 1:COLUMNS], 0.0).then_inc(columns_made, 1)

            def next_onehot(at, v, s):
                if v >= (ONE if at[1] else UNITS_OH + 2):
                    return
                if v % 2 == 0 and s == 0:
                    dve.wait_ge(ids_spread, at[0] * FILLS + (START_FILLS + v // 2))
                dve.wait_ge(onehot_used, halves(at, v) + (s + 1 - since_reuse(HALVES * v + s)))
                make_onehot(v % 2, s, HALVES * v + s)

            next_onehot((0, False), 0, 0)
            next_onehot((0, False), 0, 1)
            dve.wait_ge(w_hi_made, 1)
            dve.tensor_tensor(w2_sb[1][:, :, :], w2_raw, w2_sb[0][:, :, :].bitcast(f32), ALU.subtract)\
               .then_inc(w_lo_made, 1)
            next_onehot((0, False), 1, 0)
            dve.wait_ge(w_hi_made, 2)
            dve.tensor_tensor(w1_sb[1][0:KP, 0:3, :], w1_raw[0:KP, 0:3, :], w1_sb[0][0:KP, 0:3, :].bitcast(f32),
                              ALU.subtract).then_inc(w_lo_made, 1)
            dve.wait_ge(w_hi_made, 3)
            dve.wait_ge(w1_summed, 1)
            dve.tensor_tensor(w1_sb[1][:, 3, :], w1_raw[:, 3, :], w1_sb[0][:, 3, :].bitcast(f32), ALU.subtract)\
               .then_inc(w_lo_made, 1)
            dve.wait_ge(vectors_ready, 2 * 16)

            def run_block(at):
                def take_gram(i, u):
                    use = ("gram", i, u)
                    ps, _, free = banks(at, use)
                    wait_full(dve, at, use)
                    for n, (j, start, end) in enumerate(COPIES):
                        if n:
                            last.then_inc(dve_copied, 1)
                            dve.wait_ge(dve_copied, at[0] * COPY_WAITS + ((i * UNITS + u) * (SHARE - 1) + n))
                        last = dve.tensor_copy(gram[start:end, i, u * GRAM_UNIT + GRAM_UNIT // 2:(u + 1) * GRAM_UNIT, :],
                                               ps[start:end, GRAM_UNIT // 2:GRAM_UNIT, j * SIDE:(j + 1) * SIDE])
                    last.then_inc(free, 1)

                def split_dense(i):
                    wait_taken(dve, at, ("slots", i, 0))
                    cols = slice(i * P, (i + 1) * P)
                    dve.tensor_copy(dense_in[0][:, cols], emb_t[:, i % 2, :, 0]).then_inc(dense_hi_made, 1)
                    dve.wait_ge(dense_hi_made, at[0] * BLOCK_TILES + (i + 1))
                    dve.tensor_tensor(dense_in[1][:, cols], emb_t[:, i % 2, :, 0],
                                      dense_in[0][:, cols].bitcast(f32), ALU.subtract).then_inc(dense_lo_made, 1)

                def take_pairs(first, tiles, units):
                    lanes = tiles * QUADS
                    for n in units:
                        use = ("pairs", first, n)
                        ps, _, free = banks(at, use)
                        wait_full(dve, at, use)
                        for g, place in (x for x in unit_slots(n) if x[1] >= 4):
                            last = dve.tensor_copy(
                                pairs[0:lanes, :, pair_base(g):pair_base(g + 1)],
                                ps[0:lanes, place, 0:SHARE * SLOTS].rearrange("q (j f) -> q j f", j=SHARE)[:, :, 0:g])
                        last.then_inc(free, 1)

                def split_first_in(first, tiles):
                    lanes = tiles * QUADS
                    for k in range(3):
                        ps, _, free = bank(at, ("pairsT", first, k))
                        dve.wait_ge(pairs_hi_made, at[0] * 3 + (3 * (first // 2 if at[1] else 0) + k + 1))
                        hi_part, lo_part = (pairs_in[a][:, k, 0:tiles * P].rearrange("k (q j) -> k q j", j=SHARE)
                                            for a in range(2))
                        dve.tensor_tensor(lo_part, ps[0:KP, :, 0:lanes].rearrange("k j q -> k q j"),
                                          hi_part.bitcast(f32), ALU.subtract).then_inc(free, 1)

                def first_relu(first, tiles):
                    for n in range(2):
                        ps, _, free = banks(at, ("h1", first, n))
                        for k in range(2):
                            dve.wait_ge(h1_hi_made, at[0] * 4 + (4 * (first // 2 if at[1] else 0) + 2 * n + k + 1))
                            last = dve.scalar_tensor_tensor(
                                h1_in[1][2 * n + k][:, 0:tiles * P], row(ps[:, 4 * k:4 * k + 4, :])[:, 0:tiles * P],
                                0.0, h1_in[0][2 * n + k][:, 0:tiles * P].bitcast(f32), ALU.max, ALU.subtract)
                        last.then_inc(free, 2)

                def last_layers(first, tiles):
                    for m in range(tiles // 2):
                        use = ("h2", first, m)
                        ps, _, free = bank(at, use)
                        wait_full(dve, at, use)
                        dve.wait_ge(h2_folded, at[0] * BLOCK_TILES + (first + 1))
                        dve.tensor_tensor(h2[:, 2 * m:2 * m + 2, :], ps[:, :, :].rearrange("p (t a) c -> p t (a c)", t=2),
                                          b2_sb[:, :].unsqueeze(1).to_broadcast([P, 2, H2]), ALU.add).then_inc(free, 1)
                    for m in range(tiles // 2):
                        wait_taken(dve, at, ("h2", first, m))
                        for k in range(2):
                            tile = first + 2 * m + k
                            dve.scalar_tensor_tensor(h2[:, 2 * m + k, :], h2[:, 2 * m + k, :], 0.0, w3_sb[:, :],
                                                     ALU.max, ALU.mult,
                                                     accum_out=y_block[:, tile:tile + 1]).then_inc(h2_folded, 1)
                    dve.wait_ge(h2_folded, at[0] * BLOCK_TILES + (first + tiles + 1))
                    dve.tensor_copy(y_sb[:, bass.ds(at[0] * BLOCK_TILES + first, tiles)],
                                    y_block[:, first:first + tiles]).then_inc(y_ready, 1)

                for h in range(2):
                    i, v = 2 * h, h * ONE
                    more = not (at[1] and h == 1)
                    top = h in PARTS[at[1]]

                    def make(*which):
                        for x, s in which:
                            if more:
                                next_onehot(at, v + x, s)

                    split_dense(i)
                    if h == 0:
                        make((1, 1))
                    else:
                        make((1, 0), (1, 1))
                    take_gram(i, 0)
                    make((2, 0))
                    take_gram(i, 1)
                    make((2, 1))
                    if h == 0:
                        make((3, 0))
                    take_gram(i, 2)
                    take_gram(i, 3)
                    if h == 1:
                        make((3, 0))
                    make((3, 1))
                    split_dense(i + 1)
                    make((4, 0))
                    if not top:
                        make((4, 1))
                        take_gram(i + 1, 0)
                        make((5, 0))
                        take_gram(i + 1, 1)
                        make((5, 1))
                        take_gram(i + 1, 2)
                        make((6, 0), (6, 1), (7, 0))
                        take_gram(i + 1, 3)
                        make((7, 1))
                    else:
                        part = PARTS[at[1]][h]
                        take_gram(i + 1, 0)
                        take_gram(i + 1, 1)
                        make((4, 1))
                        take_gram(i + 1, 2)
                        take_gram(i + 1, 3)
                        make((5, 0))
                        take_pairs(*part, range(2))
                        make((5, 1))
                        take_pairs(*part, range(2, PAIR_UNITS))
                        if h == 1:
                            make((6, 0), (6, 1))
                        split_first_in(*part)
                        if h == 0:
                            make((6, 0), (6, 1))
                        first_relu(*part)
                        make((7, 0), (7, 1))
                        last_layers(*part)
                        make((8, 0))

            dve.sem_inc(h2_folded, 1)
            with dve.Fori(0, BLOCKS - 1) as b:
                run_block((b, False))
            run_block((BLOCKS - 1, True))

        @block.tensor
        def _(pe):
            for m in MAILBOXES:
                pe.sem_inc(taken[m], takers[m])
            pe.wait_ge(consts_made, 3)
            pe.wait_ge(ids_f_made, 1)

            def spread(k, table, pair):
                return pe.matmul(ids_ps[:, k, :], pick[:, table:table + 1].to_broadcast([ONE, P]), ids_f[:, bass.ds(pair * PAIR, PAIR)],
                                 start=True, stop=True)

            def multiply(ps, u, n):
                for s in range(HALVES):
                    for c in range(HALF):
                        for part in (hi, lo):
                            chunk = s * HALF + c
                            last = pe.matmul(row(ps[:, 0:2, :]), part[:, u, chunk, :],
                                             onehot[:, half_buffer(n + s), c, :],
                                             start=chunk == 0 and part is hi, stop=chunk == CHUNKS - 1 and part is lo)
                    last.then_inc(onehot_used, 1)
                    if s == 0:
                        yield

            spread(0, 0, 0)
            spread(1, 1, 0).then_inc(ids_spread, 1)
            next_fill = {1: ((2, 0), (3, 0)), 3: ((4, 0), (5, 0)), 5: ((6, 0),), 6: ((0, 1), (1, 1))}
            for u in range(ONE):
                pe.wait_ge(lo_made, u + 1)
                pe.wait_ge(taken[f"bank{u % BANKS}"], u // BANKS + 1)
                pe.wait_ge(onehot_ready, HALVES * u + 1)
                for _ in multiply(bank_ps[u % BANKS], u, HALVES * (UNITS_OH - ONE + u)):
                    pe.wait_ge(onehot_ready, HALVES * u + 2)
                    if u in next_fill:
                        for k, (table, pair) in enumerate(next_fill[u]):
                            last = spread(k, table, pair)
                        last.then_inc(ids_spread, 1)
            pe.wait_ge(columns_made, 1)

            def run_block(at):
                b, is_last = at

                def next_ids(v):
                    if is_last and v >= ONE:
                        return
                    pe.wait_ge(onehot_ready, halves(at, v))
                    pe.sem_inc(spread_begun, 1)
                    for k in range(1 if is_last and v + 1 >= ONE else 2):
                        last = spread(k, (v + k) % ONE, b * 2 + (1 + (v + k) // ONE))
                    last.then_inc(ids_spread, 1)

                def onehot_gather(v):
                    use = ("onehot", v)
                    wait_empty(pe, at, use)
                    pe.wait_ge(onehot_ready, halves(at, v) + 1)
                    for _ in multiply(bank(at, use)[0], v % ONE, HALVES * v):
                        pe.wait_ge(onehot_ready, halves(at, v) + 2)

                def transpose_tile(i):
                    early, late = 16 * (LATE - 1), 16 * (TR_SLOTS - LATE)
                    pe.wait_ge(gathered[i][0], b * early + early)
                    pe.wait_ge(dense_ready[i], b * 16 + 16)
                    for g, slots in enumerate(TR_GROUPS):
                        use = ("slots", i, g)
                        ps, ready, _ = bank(at, use)
                        if g == len(TR_GROUPS) - 1:
                            pe.wait_ge(gathered[i][1], b * late + late)
                        wait_empty(pe, at, use)
                        for s in slots:
                            last = pe.transpose(ps[:, s - slots[0], :], emb[:, i, s, :], ident[:, :])
                        last.then_inc(ready, 1)

                def gram_products(i, u):
                    use = ("gram", i, u)
                    ps, ready, _ = banks(at, use)
                    if u == 0:
                        pe.wait_ge(w_lo_made, 1)
                        for g in range(len(TR_GROUPS))[-BANKS:]:
                            wait_taken(pe, at, ("slots", i, g))
                        pe.wait_ge(moved, b * BLOCK_TILES + i + 1)
                    wait_empty(pe, at, use)
                    for k in range(GRAM_UNIT):
                        first = (u * GRAM_UNIT + k) * SHARE
                        quad = emb_t[:, i % 2, first:first + SHARE, :]
                        last = pe.matmul(ps[0:ROWS, k, 0:SHARE * SIDE], quad.rearrange("d j f -> d (j f)")[:, 0:ROWS],
                                         quad[:, :, 1:SLOTS], start=True, stop=True)
                    last.then_inc(ready, 1)

                def turn_products(first, tiles):
                    for u in (UNITS - 2, UNITS - 1):
                        wait_taken(pe, at, ("gram", first + tiles - 1, u))
                    for n in range(PAIR_UNITS):
                        use = ("pairs", first, n)
                        ps, ready, _ = banks(at, use)
                        wait_empty(pe, at, use)
                        for g, place in unit_slots(n):
                            last = pe.transpose(
                                ps[0:tiles * QUADS, place, 0:ROWS],
                                gram[0:ROWS, first:first + tiles, :, g - 1].rearrange("f t q -> f (t q)"),
                                ident[0:ROWS, 0:ROWS])
                        last.then_inc(ready, 1)

                def turn_pairs(first, tiles):
                    lanes = tiles * QUADS
                    for n in (PAIR_UNITS - 2, PAIR_UNITS - 1):
                        wait_taken(pe, at, ("pairs", first, n))
                    for k in range(3):
                        use = ("pairsT", first, k)
                        ps, ready, _ = bank(at, use)
                        wait_empty(pe, at, use)
                        for j in range(SHARE):
                            last = pe.transpose(ps[0:KP, j, 0:lanes], pairs[0:lanes, j, k * KP:(k + 1) * KP],
                                                ident[0:lanes, 0:lanes])
                        last.then_inc(ready, 1)

                def first_layer(first, tiles):
                    cols = tiles * P
                    out = [row(banks(at, ("h1", first, n // 2))[0][:, 4 * (n % 2):4 * (n % 2) + 4, :])[:, 0:cols]
                           for n in range(N1)]
                    pe.wait_ge(w_lo_made, 3)
                    pe.wait_ge(dense_lo_made, b * BLOCK_TILES + (first + tiles))
                    for n in range(N1):
                        for w, x in SPLIT_PRODUCTS:
                            pe.matmul(out[n], w1_sb[w][:, 3, n * P:(n + 1) * P], dense_in[x][:, first * P:first * P + cols],
                                      start=(w, x) == (0, 0), stop=False)
                    for k in range(3):
                        wait_taken(pe, at, ("pairsT", first, k))
                        for n in range(N1):
                            for w, x in SPLIT_PRODUCTS:
                                last = pe.matmul(out[n], w1_sb[w][0:KP, k, n * P:(n + 1) * P],
                                                 pairs_in[x][:, k, 0:cols],
                                                 start=False, stop=k == 2 and (w, x) == SPLIT_PRODUCTS[-1])
                            if k == 2 and n % 2:
                                last.then_inc(banks(at, ("h1", first, n // 2))[1], 1)

                def second_layer(first, tiles):
                    for m in range(tiles // 2):
                        wait_empty(pe, at, ("h2", first, m))
                    for t in range(2):
                        for half in range(2):
                            if t == 0:
                                wait_taken(pe, at, ("h1", first, half))
                            for m in range(tiles // 2):
                                ps, ready, _ = bank(at, ("h2", first, m))
                                s = (2 * m + t) * P
                                for k in (2 * half, 2 * half + 1):
                                    for w, x in SPLIT_PRODUCTS:
                                        last = pe.matmul(row(ps[:, 2 * t:2 * t + 2, :]), h1_in[x][k][:, s:s + P],
                                                         w2_sb[w][:, k, :], start=k == 0 and (w, x) == (0, 0),
                                                         stop=k == N1 - 1 and (w, x) == SPLIT_PRODUCTS[-1])
                                if t == 1 and half == 1:
                                    last.then_inc(ready, 1)

                for h in range(2):
                    i, v = 2 * h, h * ONE
                    more = not (is_last and h == 1)
                    top = h in PARTS[is_last]

                    def gather(*units):
                        for x in units:
                            if more:
                                onehot_gather(v + x)

                    def ids(x, here=True):
                        if more and here:
                            next_ids(v + x)

                    transpose_tile(i)
                    ids(1, h == 1)
                    gather(0)
                    gram_products(i, 0)
                    ids(2, h == 0)
                    gram_products(i, 1)
                    if not more:
                        transpose_tile(i + 1)
                    gather(1)
                    gram_products(i, 2)
                    gram_products(i, 3)
                    gather(2)
                    ids(3, h == 1)
                    if more:
                        transpose_tile(i + 1)
                    ids(4, h == 0)
                    gather(3)
                    gram_products(i + 1, 0)
                    gram_products(i + 1, 1)
                    if not top:
                        gather(4)
                        gram_products(i + 1, 2)
                        ids(6)
                        gather(5)
                        gram_products(i + 1, 3)
                        gather(6)
                    else:
                        part = PARTS[is_last][h]
                        gram_products(i + 1, 2)
                        gram_products(i + 1, 3)
                        ids(5, h == 1)
                        gather(4)
                        turn_products(*part)
                        gather(5)
                        turn_pairs(*part)
                        ids(6, h == 0)
                        first_layer(*part)
                        ids(7, h == 1)
                        gather(6)
                        second_layer(*part)

            with pe.Fori(0, BLOCKS - 1) as b:
                run_block((b, False))
            run_block((BLOCKS - 1, True))


def kernel(**inputs):
    import concourse.bacc as bacc
    from concourse.bass_utils import run_bass_kernel_spmd

    nc = bacc.Bacc("TRN2", target_bir_lowering=False, num_devices=1)
    arrays = {}

    def give(name, a):
        a = np.ascontiguousarray(a)
        arrays[name] = a
        return nc.dram_tensor(name, a.shape, mybir.dt.from_np(a.dtype), kind="ExternalInput").ap()

    ids = np.asarray(inputs["ids"])
    w1 = np.asarray(inputs["W_top1"])
    slot_feature = [0] + [1 + t for t in SLOT_TABLES]
    order = []
    for g in range(1, SLOTS):
        for f in range(g):
            i, j = sorted((slot_feature[f], slot_feature[g]))
            order.append(D + i * SLOTS - i * (i + 1) // 2 + j - i - 1)
    w1 = np.concatenate([w1[:D], w1[order], np.asarray(inputs["b_top1"])[None],
                         np.zeros((COLUMNS - PAIRS - 1, H1), w1.dtype), w1[D + PAIRS:]])
    ids_t = ids[:, ONEHOT_TABLES].reshape(P, TILES, ONE).transpose(2, 1, 0).reshape(ONE, B)
    args = [give("dense", inputs["r_dense_output"]), give("ids", ids), give("ids_t", ids_t)]
    args.append([give(f"table{t}", inputs[f"tbl_{t}"]) for t in range(TABLES)])
    args += [give("w1", w1), give("w2", inputs["W_top2"]),
             give("b2", inputs["b_top2"]), give("w3", inputs["W_top3"])]
    y = nc.dram_tensor("y", (B, 1), mybir.dt.float32, kind="ExternalOutput").ap()
    build(nc, *args, y)
    r = run_bass_kernel_spmd(nc, [arrays], core_ids=[0])
    return r.results[0]["y"]
```
